# Optimizing a Trainium2 kernel written in Bass

```python
import numpy as np
import jax
import jax.numpy as jnp

def _softmax(x, axis=-1):
    return jax.nn.softmax(x, axis=axis)

def _gelu(x):
    return jax.nn.gelu(x, approximate=True)

def _silu(x):
    return jax.nn.silu(x)

def _sigmoid(x):
    return jax.nn.sigmoid(x)

def _layernorm(x, axis=-1, eps=1e-05):
    m = jnp.mean(x, axis=axis, keepdims=True)
    v = jnp.var(x, axis=axis, keepdims=True)
    return (x - m) / jnp.sqrt(v + eps)

def _scatter_add(tgt, idx, src, axis=0):
    return tgt.at[idx].add(src)

def _segment_sum(src, seg, n):
    return jax.ops.segment_sum(src, seg, n)
kernel_name = 'mk_adaln_ffn_d1_seqx_r4_a392ab'

def setup_inputs(seed: int=0):
    np.random.seed(seed)
    _w = jnp.asarray

    def _rec_inputs():
        import jax
        import jax.numpy as jnp
        _rk = jax.random.key(seed)
        x = -7.109e-05 + 0.9999 * jax.random.normal(jax.random.fold_in(_rk, 1), (64, 64, 512), jnp.float32)
        _lenS = 64 - jax.random.randint(jax.random.fold_in(_rk, 7), (64,), 0, max(1, 64 // 4) + 1, jnp.int32)
        _lenS2 = 64 - jax.random.randint(jax.random.fold_in(_rk, 8), (64,), 0, max(1, 64 // 4) + 1, jnp.int32)
        itok_B_0_6 = jax.random.randint(jax.random.fold_in(_rk, 11), (64,), 0, 7, jnp.int32)
        return (x, itok_B_0_6)
    x, itok_B_0_6 = _rec_inputs()

    def _L0_cond_setup():
        import jax, jax.numpy as jnp
        import numpy as np
        B, T, D_IN, D_OUT = (16, 512, 512, 512)
        N_ADAPTERS, RANK = (8, 16)
        key = jax.random.key(seed)
        k_x, k_w, k_a, k_b, k_s, k_idx = jax.random.split(key, 6)
        x = jax.random.normal(k_x, (B, T, D_IN), dtype=jnp.float32)
        W = jax.random.normal(k_w, (D_OUT, D_IN), dtype=jnp.float32) * (1.0 / np.sqrt(D_IN))
        A = jax.random.normal(k_a, (N_ADAPTERS, RANK, D_IN), dtype=jnp.float32) * 0.02
        Bm = jax.random.normal(k_b, (N_ADAPTERS, D_OUT, RANK), dtype=jnp.float32) * 0.02
        scalings = jnp.ones((N_ADAPTERS,), dtype=jnp.float32)
        adapter_idx = jax.random.randint(k_idx, (B,), 0, N_ADAPTERS, dtype=jnp.int32)
        return {'x': x, 'W': W, 'A': A, 'Bm': Bm, 'scalings': scalings, 'adapter_idx': adapter_idx}
    _L0_cond_all = _L0_cond_setup()
    _L0_cond_in = {k: v for k, v in _L0_cond_all.items() if k in ('W', 'A', 'Bm', 'scalings')}
    del _L0_cond_all

    def _L0_ffn_setup():
        import jax, jax.numpy as jnp
        import numpy as np
        K_TOP = 2
        key = jax.random.key(seed)
        ks = jax.random.split(key, 6)
        s = 0.02
        B, S, H, D = (4, 256, 512, 256)
        E_SH, E_RT = (2, 16)
        return {'x': jax.random.normal(ks[0], (B, S, H), dtype=jnp.float32), 'Wsh_up': jax.random.normal(ks[1], (E_SH, H, D), dtype=jnp.float32) * s, 'Wsh_down': jax.random.normal(ks[2], (E_SH, D, H), dtype=jnp.float32) * s, 'Wrt_up': jax.random.normal(ks[3], (E_RT, H, D), dtype=jnp.float32) * s, 'Wrt_down': jax.random.normal(ks[4], (E_RT, D, H), dtype=jnp.float32) * s, 'W_router': jax.random.normal(ks[5], (H, E_RT), dtype=jnp.float32) * s}
    _L0_ffn_all = _L0_ffn_setup()
    _L0_ffn_in = {k: v for k, v in _L0_ffn_all.items() if k in ('Wsh_up', 'Wsh_down', 'Wrt_up', 'Wrt_down', 'W_router')}
    del _L0_ffn_all
    return {'x': x, 'itok_B_0_6': itok_B_0_6, 'L0_cond_W': _L0_cond_in['W'], 'L0_cond_A': _L0_cond_in['A'], 'L0_cond_Bm': _L0_cond_in['Bm'], 'L0_cond_scalings': _L0_cond_in['scalings'], 'L0_ffn_Wsh_up': _L0_ffn_in['Wsh_up'], 'L0_ffn_Wsh_down': _L0_ffn_in['Wsh_down'], 'L0_ffn_Wrt_up': _L0_ffn_in['Wrt_up'], 'L0_ffn_Wrt_down': _L0_ffn_in['Wrt_down'], 'L0_ffn_W_router': _L0_ffn_in['W_router']}

def reference(x, itok_B_0_6, L0_cond_W, L0_cond_A, L0_cond_Bm, L0_cond_scalings, L0_ffn_Wsh_up, L0_ffn_Wsh_down, L0_ffn_Wrt_up, L0_ffn_Wrt_down, L0_ffn_W_router):
    import jax
    import jax.numpy as jnp

    def _L0_cond_ref(x, W, A, Bm, scalings, adapter_idx):
        import jax, jax.numpy as jnp
        import numpy as np
        B, T, D_IN, D_OUT = (16, 512, 512, 512)
        N_ADAPTERS, RANK = (8, 16)
        H = jnp.einsum('btd,od->bto', x, W)
        A_b = A[adapter_idx]
        B_b = Bm[adapter_idx]
        s_b = scalings[adapter_idx]
        xa = jnp.einsum('btd,brd->btr', x, A_b)
        delta = jnp.einsum('btr,bor->bto', xa, B_b)
        delta = jax.lax.stop_gradient(delta * s_b[:, None, None])
        return H + delta

    def _L0_ffn_ref(x, Wsh_up, Wsh_down, Wrt_up, Wrt_down, W_router):
        import jax, jax.numpy as jnp
        import numpy as np
        K_TOP = 2
        B, S, H = x.shape
        E_rt = Wrt_up.shape[0]
        xt = x.reshape(B * S, H)
        sh_mid = jax.nn.gelu(jnp.einsum('th,ehd->ted', xt, Wsh_up), approximate=False)
        shared_out = jnp.einsum('ted,edh->th', sh_mid, Wsh_down)
        probs = jax.nn.softmax(xt @ W_router, axis=-1)
        top_v, top_i = jax.lax.top_k(probs, K_TOP)
        gate = jnp.sum(jax.nn.one_hot(top_i, E_rt, dtype=xt.dtype) * top_v[..., None], axis=1)
        rt_mid = jax.nn.gelu(jnp.einsum('th,ehd->ted', xt, Wrt_up), approximate=False)
        routed_out = jnp.einsum('ted,edh->th', rt_mid * gate[:, :, None], Wrt_down)
        return (shared_out + routed_out).reshape(B, S, H)
    x = x + _L0_ffn_ref(_L0_cond_ref(x, L0_cond_W, L0_cond_A, L0_cond_Bm, L0_cond_scalings, itok_B_0_6), L0_ffn_Wsh_up, L0_ffn_Wsh_down, L0_ffn_Wrt_up, L0_ffn_Wrt_down, L0_ffn_W_router)
    return x

_drawn_inputs = setup_inputs


def setup_inputs(seed=0):
    import zlib

    import numpy as np

    out = dict(_drawn_inputs(seed))
    spreads = {'L0_cond_scalings': (1.0, 0.6)}
    factors = {'L0_cond_A': 8.0,
     'L0_cond_Bm': 8.0,
     'L0_ffn_Wrt_up': 3.838,
     'L0_ffn_Wrt_down': 3.641,
     'L0_ffn_W_router': 3.822}
    for name, (base, spread) in spreads.items():
        noise = np.random.default_rng([zlib.crc32(name.encode()), seed]).standard_normal(out[name].shape)
        drawn = base * np.exp(spread * noise) if base else spread * noise
        out[name] = jnp.asarray(drawn.astype(out[name].dtype))
    for name, factor in factors.items():
        out[name] = (out[name] * factor).astype(out[name].dtype)
    return out
```

```python
from contextlib import ExitStack

import concourse.bass as bass
from concourse import mybir

F32 = mybir.dt.float32
BF16 = mybir.dt.bfloat16
I32 = mybir.dt.int32
U32 = mybir.dt.uint32
ALU = mybir.AluOpType
ACT = mybir.ActivationFunctionType
AX_X = mybir.AxisListType.X

P = 128
B, S, H = 64, 64, 512
TOK = B * S
HK = H // P
D = 256
DM = D // P
E_SH, E_RT = 2, 16
K_TOP = 2
N_AD, RANK = 8, 16
AR = N_AD * RANK
assert AR == P

CHUNK = 256
NT = CHUNK // P
NB = CHUNK // S
NC = TOK // CHUNK
TT = TOK // P
EM = E_SH * DM
EARLY = 4
LATE = NC - EARLY
NJ = (TOK * K_TOP + E_RT * (P - 1)) // P
NJ += NJ % 2
GRP = 8
NG = TT // GRP * K_TOP
assert EARLY == 4 and NC % 2 == 0 and NC == E_RT and EM == HK and NG == 2 * EARLY


def adaln_moe_kernel(nc, xT, x_rows, idx, WT, AT, BmT, scal, sh_up, sh_dn, rt_up, rt_dn, w_r, out):
    ctx = ExitStack()
    with ctx:
        def sb(name, shape, dt=F32):
            return ctx.enter_context(nc.sbuf_tensor(name, shape, dt))

        def sem(name):
            return ctx.enter_context(nc.semaphore(name))

        def sems(name, n=2):
            return [sem(f"{name}{s}") for s in range(n)]

        xc_dram = nc.dram_tensor("xc_dram", [TOK, H], F32, kind="Internal").ap()
        xcT_dram = nc.dram_tensor("xcT_dram", [NC, P, HK * CHUNK], F32, kind="Internal").ap()
        s_dram = nc.dram_tensor("s_dram", [TOK, H], F32, kind="Internal").ap()
        r_dram = nc.dram_tensor("r_dram", [NJ * P, H], F32, kind="Internal").ap()

        shu = sb("shu", [P, E_SH, HK, D])
        shd = sb("shd", [P, E_SH, DM, H])
        rtu = sb("rtu", [P, E_RT, HK, D])
        rtd = sb("rtd", [P, E_RT, DM, H])
        act_in = [sb(f"act_in{s}", [P, HK, CHUNK]) for s in range(2)]
        rows = [sb(f"rows{s}", [P, NT, H]) for s in range(2)]
        hid = [sb(f"hid{s}", [P, HK, CHUNK]) for s in range(2)]
        xam = [sb(f"xam{s}", [P, CHUNK]) for s in range(2)]
        xres = [sb(f"xres{s}", [P, NT, H]) for s in range(2)]
        mid = [sb(f"mid{s}", [P, D]) for s in range(2)]
        midT = [sb(f"midT{s}", [P, DM, P]) for s in range(2)]

        region = sb("region", [P, HK * H + HK * AR + H + HK * E_RT])

        def carve(sizes):
            at, views = 0, []
            for shape, dt in sizes:
                n = 1
                for d in shape:
                    n *= d
                words = n * (2 if dt is BF16 else 4) // 4
                v = region[:, at:at + words]
                at += words
                if dt is not F32:
                    v = v.bitcast(dt)
                if len(shape) == 2:
                    v = v.rearrange("p (a b) -> p a b", a=shape[0])
                elif len(shape) == 3:
                    v = v.rearrange("p (a b c) -> p a b c", a=shape[0], b=shape[1])
                views.append(v)
            assert at <= HK * H + HK * AR + H + HK * E_RT
            return views

        wt, at_, bmt, wr = carve([((HK, H), F32), ((HK, AR), F32), ((H,), F32), ((HK, E_RT), F32)])
        ex, acc0, acc1, pref, past = carve([((TT, E_RT + 1), F32), ((TT, E_RT), F32), ((TT, E_RT), F32),
                                            ((TT, E_RT), F32), ((NJ, E_RT), BF16)])
        inv_bufs = carve([((GRP, P), BF16), ((GRP, NJ), BF16), ((GRP, 2, NJ), BF16)] * 2)
        in_part, in_tile, in_val = inv_bufs[0::3], inv_bufs[1::3], inv_bufs[2::3]
        routed_bufs = carve([((H,), F32), ((HK, P), F32), ((H,), F32)] * 2)
        xg, xgT, rrow = routed_bufs[0::3], routed_bufs[1::3], routed_bufs[2::3]
        c_s, c_r0, c_r1 = xg, [v.rearrange("p a b -> p (a b)") for v in xgT], rrow

        ident = sb("ident", [P, P])
        lower = sb("lower", [P, P], BF16)
        ones = sb("ones", [P, P], BF16)
        iota_p = sb("iota_p", [P, P], BF16)
        iota_j = sb("iota_j", [P, NJ])
        iota_e = sb("iota_e", [P, E_RT])
        tile_no = sb("tile_no", [P, TT])
        part_i = sb("part_i", [P, 1], I32)
        part_f = sb("part_f", [P, 1])
        ad_i = sb("ad_i", [P, 1], I32)
        ad_f = sb("ad_f", [P, 1])
        sc_col = sb("sc_col", [P, 1])
        idx_b = sb("idx_b", [P, B], I32)
        mask = sb("mask", [P, B])
        lg = sb("lg", [P, TT, E_RT])
        lg_c = [sb(f"lg_c{s}", [P, NT, E_RT]) for s in range(2)]
        best_c = [sb(f"best_c{s}", [P, NT, 8]) for s in range(2)]
        best_i_c = [sb(f"best_i_c{s}", [P, NT, 8], U32) for s in range(2)]
        best = sb("best", [P, TT, K_TOP])
        zsum = sb("zsum", [P, TT])
        gate = sb("gate", [P, K_TOP, TT])
        chosen = sb("chosen", [P, K_TOP, TT])
        oh = [sb(f"oh{r}", [P, TT, E_RT], BF16) for r in range(K_TOP)]
        oh_sum = sb("oh_sum", [P, TT, E_RT], BF16)
        cnt_i = sb("cnt_i", [P, E_RT], I32)
        tiles_i = sb("tiles_i", [P, E_RT], I32)
        tiles_f = sb("tiles_f", [P, E_RT])
        end_t = [sb(f"end_t{s}", [P, E_RT]) for s in range(2)]
        start_s = sb("start_s", [P, E_RT])
        pos_f = sb("pos_f", [P, K_TOP, TT])
        pos = sb("pos", [P, K_TOP, TT], I32)
        hi_i = sb("hi_i", [P, K_TOP, TT], I32)
        lo_i = sb("lo_i", [P, K_TOP, TT], I32)
        hi_f = sb("hi_f", [P, K_TOP, TT])
        lo_f = sb("lo_f", [P, K_TOP, TT])
        tile_e_f = sb("tile_e_f", [P, NJ])
        tile_e = sb("tile_e", [P, NJ], I32)
        tok_f = sb("tok_f", [P, NJ])
        tok = sb("tok", [P, NJ], I32)
        slot_idx = [sb(f"slot_idx{s}", [P, 1], I32) for s in range(2)]
        row_idx = [sb(f"row_idx{s}", [P, K_TOP], I32) for s in range(2)]

        bank = [ctx.enter_context(nc.psum_tensor(f"bank{i}", [P, 512], F32)) for i in range(8)]
        XA, COND, XPOSE, LOGIT = bank[0], bank[1:3], bank[3:5], bank[5]
        PRE, TOT, INV = bank[6], bank[7], bank[0]
        UP, DOWN = bank[1:3], bank[3:5]
        R_XT, R_UP, R_MT, R_DN = [bank[0], bank[5]], bank[6:8], bank[1:3], bank[3:5]

        w_cond, w_shared, w_routed = sem("w_cond"), sem("w_shared"), sem("w_routed")
        iotas, masks, consts = sem("iotas"), sem("masks"), sem("consts")
        v_step = sem("v_step")
        act_loaded, act_used = sems("act_loaded"), sem("act_used")
        xa_ready, xam_ready = sem("xa_ready"), sem("xam_ready")
        cond_ready, rows_ready = sem("cond_ready"), sem("rows_ready")
        xpose_ready, condT_ready = sem("xpose_ready"), sem("condT_ready")
        rows_stored, condT_stored = sems("rows_stored"), sems("condT_stored")
        logit_ready, logit_copied, best_ready = sem("logit_ready"), sem("logit_copied"), sem("best_ready")
        place_found, top_ready = sem("place_found"), sem("top_ready")
        onehot_ready, prefix_ready = sem("onehot_ready"), sem("prefix_ready")
        shifted_ready, exp_ready = sem("shifted_ready"), sem("exp_ready")
        place_ready, place_used, sorted_ready = sem("place_ready"), sem("place_used"), sem("sorted_ready")
        up_ready, gelu_ready = sem("up_ready"), sem("gelu_ready")
        down_ready, shared_ready = sem("down_ready"), sem("shared_ready")
        x_loaded, sum_ready = sems("x_loaded"), sem("sum_ready")
        idx_first, idx_ready = sem("idx_first"), sem("idx_ready")
        xg_loaded = sems("xg_loaded")
        xgT_psum, xgT_ready = sem("xgT_psum"), sem("xgT_ready")
        r_up_ready, r_gelu_ready = sem("r_up_ready"), sem("r_gelu_ready")
        midT_psum, midT_ready = sem("midT_psum"), sem("midT_ready")
        r_dn_ready, rrow_ready = sem("r_dn_ready"), sem("rrow_ready")
        rrow_stored = sems("rrow_stored")
        c_idx_first, c_idx_ready = sem("c_idx_first"), sem("c_idx_ready")
        c_s_loaded, c_r_loaded = sems("c_s_loaded"), sems("c_r_loaded")
        c_half, c_ready, c_stored = sem("c_half"), sem("c_ready"), sems("c_stored")

        block = ctx.enter_context(nc.Block())

        def flat(ap):
            return ap.rearrange("p k t -> p (k t)")

        def chunk_rows(dram, c):
            return dram[bass.ds(c * CHUNK, CHUNK), :].rearrange("(t p) h -> p t h", p=P)

        def chunk_T(dram, c):
            return dram[bass.ds(c, 1)].rearrange("a p n -> p (a n)")

        def tile_rows(dram, n):
            return dram[bass.ds(n * P, P), :]

        A_HALF = NC // 2

        @block.sync
        def _(sp):
            for dst, src in ((at_, AT), (wt, WT), (bmt, BmT), (wr, w_r)):
                sp.dma_start(dst, src).then_inc(w_cond, 16)
            sp.dma_start(sc_col[:], scal).then_inc(w_cond, 16)
            sp.dma_start(idx_b[:], idx.partition_broadcast(P)).then_inc(w_cond, 16)
            for c in range(2):
                sp.dma_start(flat(act_in[c][:]), chunk_T(xT, c)).then_inc(act_loaded[c], 16)
            sp.dma_start(shu[:], sh_up).then_inc(w_shared, 16)
            sp.dma_start(shd[:], sh_dn).then_inc(w_shared, 16)

            def cond_chunk(i, s, more):
                c = 2 * i + s
                sp.dma_start(rtu[:, bass.ds(c, 1)], rt_up[:, bass.ds(c, 1)]).then_inc(w_routed, 16)
                sp.dma_start(rtd[:, bass.ds(c, 1)], rt_dn[:, bass.ds(c, 1)]).then_inc(w_routed, 16)
                if more:
                    sp.wait_ge(act_used, c + 1)
                    sp.dma_start(flat(act_in[s][:]), chunk_T(xT, c + 2)).then_inc(act_loaded[s], 16)
                sp.wait_ge(rows_ready, NT * c + NT)
                sp.dma_start(chunk_rows(xc_dram, c), rows[s][:]).then_inc(rows_stored[s], 16)
                sp.wait_ge(condT_ready, NT * c + NT)
                sp.dma_start(chunk_T(xcT_dram, c), flat(hid[s][:])).then_inc(condT_stored[s], 16)

            with sp.Fori(0, A_HALF - 1) as i:
                for s in range(2):
                    cond_chunk(i, s, True)
            for s in range(2):
                cond_chunk(A_HALF - 1, s, False)

            def load_condT(c, s):
                sp.dma_start(flat(act_in[s][:]), chunk_T(xcT_dram, c)).then_inc(act_loaded[s], 16)

            def load_x(c, s):
                sp.dma_start(xres[s][:], chunk_rows(x_rows, c)).then_inc(x_loaded[s], 16)

            for s in range(2):
                load_x(s, s)
                sp.wait_ge(act_used, NC)
                sp.wait_ge(condT_stored[s], 16 * A_HALF)
                load_condT(s, s)

            def shared_chunk(i, s, more):
                c = 2 * i + s
                if more:
                    sp.wait_ge(up_ready, EM * c + EM)
                    load_condT(c + 2, s)
                sp.wait_ge(sum_ready, c + 1)
                sp.dma_start(chunk_rows(s_dram, c), rows[s][:]).then_inc(rows_stored[s], 16)
                if more:
                    load_x(c + 2, s)

            with sp.Fori(0, EARLY // 2) as i:
                for s in range(2):
                    shared_chunk(i, s, True)

            with sp.Fori(0, NJ // 2) as i:
                for s in range(2):
                    j = 2 * i + s
                    sp.wait_ge(rrow_ready, j + 1)
                    sp.dma_start(tile_rows(r_dram, j), rrow[s]).then_inc(rrow_stored[s], 16)

            def sum_loads(k, first=False):
                for s in range(2):
                    n = 2 * k + s
                    if not first:
                        sp.wait_ge(c_stored[s], 16 * k)
                    sp.dma_start(c_s[s], tile_rows(s_dram, n)).then_inc(c_s_loaded[s], 16)

            def sum_stores(k):
                for s in range(2):
                    n = 2 * k + s
                    sp.wait_ge(c_ready, n + 1)
                    sp.dma_start(tile_rows(out, n), c_s[s]).then_inc(c_stored[s], 16)

            def late_chunk(i, s, more, first=False):
                k = 2 * i + s - EARLY
                sp.wait_ge(rows_stored[s], 16 * (A_HALF + i - EARLY // 2 + 1))
                sum_loads(k, first)
                shared_chunk(i, s, more)
                sum_stores(k)

            sp.wait_ge(xgT_psum, NJ)
            for s in range(2):
                late_chunk(EARLY // 2, s, True, first=(s == 0))
            with sp.Fori(EARLY // 2 + 1, A_HALF - 1) as i:
                for s in range(2):
                    late_chunk(i, s, True)
            for s in range(2):
                late_chunk(A_HALF - 1, s, False)
            for k in range(LATE, NC):
                sp.wait_ge(rows_stored[k % 2], 16 * (A_HALF + k // 2 + 1))
                sum_loads(k)
                sum_stores(k)
            for s in range(2):
                sp.wait_ge(c_stored[s], 16 * NC)

        @block.gpsimd
        def _(pool):
            def iota(dst, n):
                nc.gpsimd.iota(dst, [[1, n]], base=0, channel_multiplier=0,
                               allow_small_or_imprecise_dtypes=True).then_inc(iotas, 1)

            nc.gpsimd.iota(part_i[:], [[0, 1]], base=0, channel_multiplier=1).then_inc(iotas, 1)
            iota(iota_p[:], P)
            iota(iota_j[:], NJ)
            iota(iota_e[:], E_RT)
            iota(tile_no[:], TT)
            nc.gpsimd.memset(ident[:], 0.0).then_inc(masks, 1)
            nc.gpsimd.memset(ones[:], 1.0).then_inc(masks, 1)
            nc.gpsimd.memset(lower[:], 1.0).then_inc(masks, 1)
            pool.wait_ge(masks, 3)
            nc.gpsimd.affine_select(out=ident[:], in_=ident[:], compare_op=ALU.not_equal, fill=1.0, base=0,
                                    pattern=[[-1, P]], channel_multiplier=1).then_inc(consts, 1)
            nc.gpsimd.affine_select(out=lower[:], in_=lower[:], compare_op=ALU.is_gt, fill=0.0, base=0,
                                    pattern=[[1, P]], channel_multiplier=-1).then_inc(consts, 1)

            def add_x(i, s):
                c = 2 * i + s
                pool.wait_ge(shared_ready, NT * c + NT)
                pool.wait_ge(x_loaded[s], 16 * (i + 1))
                nc.gpsimd.tensor_tensor(rows[s][:], rows[s][:], xres[s][:], ALU.add).then_inc(sum_ready, 1)

            with pool.Fori(0, EARLY // 2) as i:
                for s in range(2):
                    add_x(i, s)

            pool.wait_ge(sorted_ready, 1)
            for s in range(2):
                pool.wait_ge(rows_stored[s], 16 * A_HALF)

            def gather(i, s, first):
                j = 2 * i + s
                copied = idx_first if first else idx_ready
                if not first:
                    pool.wait_ge(xgT_psum, j - 1)
                nc.gpsimd.tensor_copy(slot_idx[s][:], tok[:, bass.ds(j, 1)]).then_inc(copied, 1)
                pool.wait_ge(sorted_ready, 1)
                pool.wait_ge(copied, j + 1 if first else j - 1)
                nc.gpsimd.indirect_dma_start(
                    out=xg[s], out_offset=None, in_=xc_dram,
                    in_offset=bass.IndirectOffsetOnAxis(ap=slot_idx[s][:].bitcast(U32), axis=0),
                ).then_inc(xg_loaded[s], 16)

            for s in range(2):
                gather(0, s, True)
            with pool.Fori(1, NJ // 2) as i:
                for s in range(2):
                    gather(i, s, False)

            def gather_back(k, first):
                copied = c_idx_first if first else c_idx_ready
                for s in range(2):
                    n = 2 * k + s
                    if not first:
                        pool.wait_ge(c_ready, n - 1)
                    nc.gpsimd.tensor_copy(row_idx[s][:], pos[:, :, bass.ds(n, 1)].rearrange("p r a -> p (r a)")).then_inc(copied, 1)
                    pool.wait_ge(sorted_ready, 1)
                    pool.wait_ge(copied, n + 1 if first else n - 1)
                    for r, dst in enumerate((c_r0, c_r1)):
                        nc.gpsimd.indirect_dma_start(
                            out=dst[s], out_offset=None, in_=r_dram,
                            in_offset=bass.IndirectOffsetOnAxis(ap=row_idx[s][:, r:r + 1].bitcast(U32), axis=0),
                        ).then_inc(c_r_loaded[s], 16)

            pool.wait_ge(r_up_ready, NJ)
            for s in range(2):
                pool.wait_ge(rrow_stored[s], 16 * (NJ // 2))
            for s in range(2):
                gather_back(s, s == 0)
                add_x(EARLY // 2, s)
            with pool.Fori(EARLY // 2 + 1, A_HALF) as i:
                for s in range(2):
                    gather_back(2 * i + s - EARLY, False)
                    add_x(i, s)
            for k in range(LATE, NC):
                gather_back(k, False)

        @block.scalar
        def _(act):
            def cond_rows(i, s, first=False):
                c = 2 * i + s
                if not first:
                    act.wait_ge(rows_stored[s], 16 * i)
                for t in range(NT):
                    act.wait_ge(cond_ready, NT * c + t + 1)
                    nc.scalar.copy(rows[s][:, t, :], COND[t][:]).then_inc(rows_ready, 1)

            for s in range(2):
                cond_rows(0, s, first=True)
            with act.Fori(1, A_HALF) as i:
                for s in range(2):
                    cond_rows(i, s)

            act.wait_ge(shifted_ready, 1)
            nc.scalar.activation(ex, ex, ACT.Exp).then_inc(exp_ready, 1)

            def gelus(i, s):
                c = 2 * i + s
                for em in range(EM):
                    act.wait_ge(up_ready, EM * c + em + 1)
                    nc.scalar.activation(hid[s][:, em, :], UP[em % 2][:, 0:CHUNK], ACT.Gelu).then_inc(gelu_ready, 1)

            def shared_rows(i, s):
                c = 2 * i + s
                act.wait_ge(rows_stored[s], 16 * (A_HALF + i))
                for t in range(NT):
                    act.wait_ge(down_ready, NT * c + t + 1)
                    nc.scalar.copy(rows[s][:, t, :], DOWN[t][:]).then_inc(shared_ready, 1)

            def shared_phase(i0, i1):
                gelus(i0, 0)
                with act.Fori(i0, i1 - 1) as i:
                    gelus(i, 1)
                    shared_rows(i, 0)
                    gelus(i + 1, 0)
                    shared_rows(i, 1)
                gelus(i1 - 1, 1)
                shared_rows(i1 - 1, 0)
                shared_rows(i1 - 1, 1)

            for s in range(2):
                act.wait_ge(condT_stored[s], 16 * A_HALF)
            shared_phase(0, EARLY // 2)

            def r_gelu(j, s):
                act.wait_ge(r_up_ready, j + 1)
                nc.scalar.activation(mid[s][:], R_UP[s][:, 0:D], ACT.Gelu).then_inc(r_gelu_ready, 1)

            def r_rows(j, i, s, first=False):
                if not first:
                    act.wait_ge(rrow_stored[s], 16 * i)
                act.wait_ge(r_dn_ready, j + 1)
                nc.scalar.copy(rrow[s], R_DN[s][:]).then_inc(rrow_ready, 1)

            r_gelu(0, 0)
            r_gelu(1, 1)
            r_rows(0, 0, 0, first=True)
            r_gelu(2, 0)
            r_rows(1, 0, 1, first=True)
            with act.Fori(1, NJ // 2 - 1) as i:
                r_gelu(2 * i + 1, 1)
                r_rows(2 * i, i, 0)
                r_gelu(2 * i + 2, 0)
                r_rows(2 * i + 1, i, 1)
            r_gelu(NJ - 1, 1)
            r_rows(NJ - 2, NJ // 2 - 1, 0)
            r_rows(NJ - 1, NJ // 2 - 1, 1)

            shared_phase(EARLY // 2, A_HALF)

        @block.vector
        def _(dve):
            steps = [0]

            def link(ins):
                steps[0] += 1
                ins.then_inc(v_step, 1)
                dve.wait_ge(v_step, steps[0])

            dve.wait_ge(w_cond, 6 * 16)
            dve.wait_ge(iotas, 5)
            link(nc.vector.tensor_scalar(ad_i[:], part_i[:], RANK.bit_length() - 1, None, ALU.logical_shift_right))
            link(nc.vector.tensor_copy(ad_f[:], ad_i[:]))
            link(nc.vector.tensor_copy(part_f[:], part_i[:]))
            link(nc.vector.tensor_scalar(mask[:], idx_b[:], ad_f[:], sc_col[:], ALU.is_equal, ALU.mult))

            def mask_xa(c, s):
                dve.wait_ge(xa_ready, c + 1)
                nc.vector.tensor_tensor(
                    xam[s][:].rearrange("p (b t) -> p b t", b=NB), XA[:, 0:CHUNK].rearrange("p (b t) -> p b t", b=NB),
                    mask[:, bass.ds(c * NB, NB)].unsqueeze(2).to_broadcast([P, NB, S]), ALU.mult,
                ).then_inc(xam_ready, 1)

            def cond_T(c, i, s, first=False):
                if not first:
                    dve.wait_ge(condT_stored[s], 16 * i)
                for t in range(NT):
                    dve.wait_ge(xpose_ready, NT * c + t + 1)
                    nc.vector.tensor_copy(hid[s][:, :, t * P:(t + 1) * P],
                                          XPOSE[t][:].rearrange("p (k t) -> p k t", k=HK)).then_inc(condT_ready, 1)

            def top(c, s):
                dve.wait_ge(logit_ready, c + 1)
                nc.vector.tensor_copy(lg_c[s][:], LOGIT[:, 0:NT * E_RT].rearrange("p (t e) -> p t e", t=NT)).then_inc(logit_copied, 1)
                dve.wait_ge(logit_copied, c + 1)
                nc.vector.tensor_copy(lg[:, bass.ds(c * NT, NT), :], lg_c[s][:])
                for t in range(NT):
                    nc.vector.max(best_c[s][:, t, :], lg_c[s][:, t, :]).then_inc(best_ready, 1)
                dve.wait_ge(best_ready, c * NT + NT)
                nc.vector.tensor_copy(best[:, bass.ds(c * NT, NT), :], best_c[s][:, :, 0:K_TOP])
                for t in range(NT):
                    nc.vector.max_index(best_i_c[s][:, t, :], best_c[s][:, t, :], lg_c[s][:, t, :]).then_inc(place_found, 1)
                dve.wait_ge(place_found, c * NT + NT)
                nc.vector.tensor_copy(chosen[:, :, bass.ds(c * NT, NT)],
                                      best_i_c[s][:, :, 0:K_TOP].rearrange("p t r -> p r t")).then_inc(top_ready, 1)

            mask_xa(0, 0)
            mask_xa(1, 1)
            cond_T(0, 0, 0, first=True)
            top(0, 0)
            mask_xa(2, 0)
            cond_T(1, 0, 1, first=True)
            top(1, 1)
            with dve.Fori(1, A_HALF - 1) as i:
                mask_xa(2 * i + 1, 1)
                cond_T(2 * i, i, 0)
                top(2 * i, 0)
                mask_xa(2 * i + 2, 0)
                cond_T(2 * i + 1, i, 1)
                top(2 * i + 1, 1)
            mask_xa(NC - 1, 1)
            cond_T(NC - 2, A_HALF - 1, 0)
            top(NC - 2, 0)
            cond_T(NC - 1, A_HALF - 1, 1)
            top(NC - 1, 1)
            dve.wait_ge(top_ready, NC)

            nc.vector.tensor_tensor(ex[:, :, 0:E_RT], lg[:], best[:, :, 0:1].to_broadcast([P, TT, E_RT]), ALU.subtract)
            nc.vector.tensor_tensor(ex[:, :, E_RT:E_RT + 1], best[:, :, 1:2], best[:, :, 0:1],
                                    ALU.subtract).then_inc(shifted_ready, 1)
            for r in range(K_TOP):
                link(nc.vector.tensor_tensor(oh[r][:], iota_e[:].unsqueeze(1).to_broadcast([P, TT, E_RT]),
                                             chosen[:, r, :].unsqueeze(2).to_broadcast([P, TT, E_RT]), ALU.is_equal))
            nc.vector.tensor_tensor(oh_sum[:], oh[0][:], oh[1][:], ALU.add).then_inc(onehot_ready, 1)

            dve.wait_ge(exp_ready, 1)
            link(nc.vector.tensor_reduce(zsum[:], ex[:, :, 0:E_RT], AX_X, ALU.add))
            link(nc.vector.reciprocal(gate[:, 0, :], zsum[:]))
            link(nc.vector.tensor_tensor(gate[:, 1, :], gate[:, 0, :], ex[:, :, E_RT], ALU.mult))

            dve.wait_ge(prefix_ready, 1)
            link(nc.vector.tensor_copy(acc0, TOT[:].rearrange("p (t e) -> p t e", t=TT)))
            src, dst, d = acc0, acc1, 1
            while d < TT:
                nc.vector.tensor_copy(dst[:, 0:d, :], src[:, 0:d, :])
                link(nc.vector.tensor_tensor(dst[:, d:, :], src[:, d:, :], src[:, :TT - d, :], ALU.add))
                src, dst, d = dst, src, 2 * d
            link(nc.vector.tensor_scalar(cnt_i[:], src[:, TT - 1, :], float(P - 1), None, ALU.add))
            link(nc.vector.tensor_scalar(tiles_i[:], cnt_i[:], P.bit_length() - 1, None, ALU.logical_shift_right))
            link(nc.vector.tensor_copy(tiles_f[:], tiles_i[:]))
            link(nc.vector.tensor_copy(end_t[0][:], tiles_f[:]))
            a, b, d = end_t[0], end_t[1], 1
            while d < E_RT:
                nc.vector.tensor_copy(b[:, 0:d], a[:, 0:d])
                link(nc.vector.tensor_tensor(b[:, d:], a[:, d:], a[:, :E_RT - d], ALU.add))
                a, b, d = b, a, 2 * d
            link(nc.vector.tensor_tensor(start_s[:], a[:], tiles_f[:], ALU.subtract))
            link(nc.vector.tensor_scalar(start_s[:], start_s[:], float(P), None, ALU.mult))
            link(nc.vector.tensor_tensor(past, iota_j[:].unsqueeze(2).to_broadcast([P, NJ, E_RT]),
                                         a[:].unsqueeze(1).to_broadcast([P, NJ, E_RT]), ALU.is_ge))
            link(nc.vector.tensor_reduce(tile_e_f[:], past, AX_X, ALU.add))
            link(nc.vector.tensor_scalar(tile_e[:], tile_e_f[:], float(E_RT - 1), None, ALU.min))
            link(nc.vector.tensor_tensor(dst, src, TOT[:].rearrange("p (t e) -> p t e", t=TT), ALU.subtract))
            link(nc.vector.tensor_tensor(pref, dst, PRE[:].rearrange("p (t e) -> p t e", t=TT), ALU.add))
            link(nc.vector.tensor_tensor(pref, pref, start_s[:].unsqueeze(1).to_broadcast([P, TT, E_RT]), ALU.add))
            for r in range(K_TOP):
                link(nc.vector.tensor_tensor(acc0, oh[r][:], pref, ALU.mult))
                link(nc.vector.tensor_reduce(pos_f[:, r, :], acc0, AX_X, ALU.add))
            link(nc.vector.tensor_copy(pos[:], pos_f[:]))
            link(nc.vector.tensor_scalar(hi_i[:], pos[:], P.bit_length() - 1, None, ALU.logical_shift_right))
            link(nc.vector.tensor_scalar(lo_i[:], pos[:], P - 1, None, ALU.bitwise_and))
            link(nc.vector.tensor_copy(hi_f[:], hi_i[:]))
            link(nc.vector.tensor_copy(lo_f[:], lo_i[:]))

            for g in range(NG):
                s, r, n0 = g % 2, g % K_TOP, g // K_TOP * GRP
                if g >= 2:
                    dve.wait_ge(place_used, g - 1)
                nc.vector.tensor_tensor(in_part[s], iota_p[:].unsqueeze(1).to_broadcast([P, GRP, P]),
                                        lo_f[:, r, n0:n0 + GRP].unsqueeze(2).to_broadcast([P, GRP, P]), ALU.is_equal)
                link(nc.vector.tensor_tensor(in_tile[s], iota_j[:].unsqueeze(1).to_broadcast([P, GRP, NJ]),
                                             hi_f[:, r, n0:n0 + GRP].unsqueeze(2).to_broadcast([P, GRP, NJ]), ALU.is_equal))
                nc.vector.tensor_tensor(in_val[s][:, :, 0, :], in_tile[s],
                                        tile_no[:, n0:n0 + GRP].unsqueeze(2).to_broadcast([P, GRP, NJ]), ALU.mult)
                nc.vector.tensor_scalar(in_val[s][:, :, 1, :], in_tile[s], part_f[:], None,
                                        ALU.mult).then_inc(place_ready, 1)
            dve.wait_ge(place_used, NG)
            link(nc.vector.tensor_scalar(tok_f[:], INV[:, 0:NJ], float(P), None, ALU.mult))
            nc.vector.tensor_tensor(tok[:], tok_f[:], INV[:, NJ:2 * NJ], ALU.add).then_inc(sorted_ready, 1)

            def copy_xgT(j, s):
                dve.wait_ge(xgT_psum, j + 1)
                nc.vector.tensor_copy(xgT[s], R_XT[s][:].rearrange("p (k t) -> p k t", k=HK)).then_inc(xgT_ready, 1)

            def copy_midT(j, s):
                dve.wait_ge(midT_psum, j + 1)
                nc.vector.tensor_copy(midT[s][:], R_MT[s][:, 0:D].rearrange("p (m t) -> p m t", m=DM)).then_inc(midT_ready, 1)

            copy_xgT(0, 0)
            with dve.Fori(0, NJ // 2 - 1) as i:
                copy_xgT(2 * i + 1, 1)
                copy_midT(2 * i, 0)
                copy_xgT(2 * i + 2, 0)
                copy_midT(2 * i + 1, 1)
            copy_xgT(NJ - 1, 1)
            copy_midT(NJ - 2, 0)
            copy_midT(NJ - 1, 1)

            with dve.Fori(0, TT // 2) as i:
                for s in range(2):
                    n = 2 * i + s
                    dve.wait_ge(c_s_loaded[s], 16 * (i + 1))
                    dve.wait_ge(c_r_loaded[s], K_TOP * 16 * (i + 1))
                    nc.vector.scalar_tensor_tensor(c_s[s], c_r0[s], gate[:, 0, bass.ds(n, 1)], c_s[s],
                                                   ALU.mult, ALU.add).then_inc(c_half, 1)
                    dve.wait_ge(c_half, n + 1)
                    nc.vector.scalar_tensor_tensor(c_s[s], c_r1[s], gate[:, 1, bass.ds(n, 1)], c_s[s],
                                                   ALU.mult, ALU.add).then_inc(c_ready, 1)

        @block.tensor
        def _(pe):
            mm = nc.tensor.matmul

            def cond_products(c, i, s, first=False):
                pe.wait_ge(act_loaded[s], 16 * (i + 1))
                if not first:
                    pe.wait_ge(xam_ready, c)
                for k in range(HK):
                    last = mm(XA[:, 0:CHUNK], at_[:, k, :], act_in[s][:, k, :], start=(k == 0), stop=(k == HK - 1))
                last.then_inc(xa_ready, 1)
                for t in range(NT):
                    if not first:
                        pe.wait_ge(rows_ready, NT * c - NT + t + 1)
                    for k in range(HK):
                        last = mm(COND[t][:], act_in[s][:, k, t * P:(t + 1) * P], wt[:, k, :], start=(k == 0), stop=False)
                last.then_inc(act_used, 1)

            def adapter_products(c, s):
                pe.wait_ge(xam_ready, c + 1)
                for t in range(NT):
                    mm(COND[t][:], xam[s][:, t * P:(t + 1) * P], bmt, start=False, stop=True).then_inc(cond_ready, 1)

            def cond_transposes(c, s, first=False):
                for t in range(NT):
                    pe.wait_ge(rows_ready, NT * c + t + 1)
                    if not first:
                        pe.wait_ge(condT_ready, NT * c - NT + t + 1)
                    for k in range(HK):
                        last = nc.tensor.transpose(XPOSE[t][:, k * P:(k + 1) * P], rows[s][:, t, k * P:(k + 1) * P], ident[:])
                    last.then_inc(xpose_ready, 1)

            def router_products(c, s, first=False):
                pe.wait_ge(condT_ready, NT * c + NT)
                if not first:
                    pe.wait_ge(logit_copied, c)
                for t in range(NT):
                    for k in range(HK):
                        last = mm(LOGIT[:, t * E_RT:(t + 1) * E_RT], hid[s][:, k, t * P:(t + 1) * P], wr[:, k, :],
                                  start=(k == 0), stop=(k == HK - 1))
                last.then_inc(logit_ready, 1)

            def cond_step(c, i, s, first=False):
                cond_products(c, i, s)
                cond_transposes(c - 1, 1 - s, first)
                adapter_products(c, s)
                router_products(c - 1, 1 - s, first)

            pe.wait_ge(w_cond, 6 * 16)
            pe.wait_ge(consts, 2)
            cond_products(0, 0, 0, first=True)
            adapter_products(0, 0)
            cond_step(1, 0, 1, first=True)
            with pe.Fori(1, A_HALF) as i:
                cond_step(2 * i, i, 0)
                cond_step(2 * i + 1, i, 1)
            cond_transposes(NC - 1, 1)
            router_products(NC - 1, 1)

            def prefix_products():
                pe.wait_ge(onehot_ready, 1)
                mm(PRE[:], lower[:], oh_sum[:].rearrange("p t e -> p (t e)"), start=True, stop=True)
                mm(TOT[:], ones[:], oh_sum[:].rearrange("p t e -> p (t e)"), start=True, stop=True).then_inc(prefix_ready, 1)

            def inversion_products(g):
                pe.wait_ge(place_ready, g + 1)
                for n in range(GRP):
                    last = mm(INV[:, 0:2 * NJ], in_part[g % 2][:, n, :], in_val[g % 2][:, n, :, :].rearrange("p a j -> p (a j)"),
                              start=(g == 0 and n == 0), stop=(g == NG - 1 and n == GRP - 1))
                last.then_inc(place_used, 1)

            def shared_up(i, s, first=False):
                c = 2 * i + s
                pe.wait_ge(act_loaded[s], 16 * (A_HALF + i + 1))
                for em in range(EM):
                    e, m = em // DM, em % DM
                    if not (first and em < 2):
                        pe.wait_ge(gelu_ready, EM * c + em - 1)
                    for k in range(HK):
                        last = mm(UP[em % 2][:, 0:CHUNK], shu[:, e, k, m * P:(m + 1) * P], act_in[s][:, k, :],
                                  start=(k == 0), stop=(k == HK - 1))
                    last.then_inc(up_ready, 1)

            def shared_down(i, s, first=False):
                c = 2 * i + s
                pe.wait_ge(gelu_ready, EM * c + EM)
                for t in range(NT):
                    if not first:
                        pe.wait_ge(shared_ready, NT * c - NT + t + 1)
                    for em in range(EM):
                        last = mm(DOWN[t][:], hid[s][:, em, t * P:(t + 1) * P], shd[:, em // DM, em % DM, :],
                                  start=(em == 0), stop=(em == EM - 1))
                    last.then_inc(down_ready, 1)

            pe.wait_ge(w_shared, 2 * 16)
            pe.wait_ge(rows_ready, TT)
            shared_up(0, 0, first=True)
            prefix_products()
            shared_up(0, 1)
            shared_down(0, 0, first=True)
            shared_up(1, 0)
            inversion_products(0)
            inversion_products(1)
            shared_down(0, 1)
            inversion_products(2)
            inversion_products(3)
            shared_up(1, 1)
            inversion_products(4)
            inversion_products(5)
            shared_down(1, 0)
            inversion_products(6)
            inversion_products(7)
            shared_down(1, 1)

            def r_transpose_x(j, i, s, first=False):
                pe.wait_ge(xg_loaded[s], 16 * (i + 1))
                if not first:
                    pe.wait_ge(xgT_ready, j - 1)
                for k in range(HK):
                    last = nc.tensor.transpose(R_XT[s][:, k * P:(k + 1) * P], xg[s][:, k * P:(k + 1) * P], ident[:])
                last.then_inc(xgT_psum, 1)

            def r_up(j, s, first=False):
                e = pe.value_load(tile_e[0:1, bass.ds(j, 1)], min_val=0, max_val=E_RT - 1)
                pe.wait_ge(xgT_ready, j + 1)
                if not first:
                    pe.wait_ge(r_gelu_ready, j - 1)
                for k in range(HK):
                    last = mm(R_UP[s][:, 0:D], xgT[s][:, k, :], rtu[:, bass.ds(e, 1), k, :].rearrange("p a d -> p (a d)"),
                              start=(k == 0), stop=(k == HK - 1))
                last.then_inc(r_up_ready, 1)

            def r_transpose_mid(j, s, first=False):
                pe.wait_ge(r_gelu_ready, j + 1)
                if not first:
                    pe.wait_ge(midT_ready, j - 1)
                for m in range(DM):
                    last = nc.tensor.transpose(R_MT[s][:, m * P:(m + 1) * P], mid[s][:, m * P:(m + 1) * P], ident[:])
                last.then_inc(midT_psum, 1)

            def r_down(j, s, first=False):
                e = pe.value_load(tile_e[0:1, bass.ds(j, 1)], min_val=0, max_val=E_RT - 1)
                pe.wait_ge(midT_ready, j + 1)
                if not first:
                    pe.wait_ge(rrow_ready, j - 1)
                for m in range(DM):
                    last = mm(R_DN[s][:], midT[s][:, m, :], rtd[:, bass.ds(e, 1), m, :].rearrange("p a h -> p (a h)"),
                              start=(m == 0), stop=(m == DM - 1))
                last.then_inc(r_dn_ready, 1)

            pe.wait_ge(w_routed, 2 * E_RT * 16)
            pe.wait_ge(sorted_ready, 1)
            pe.wait_ge(shared_ready, NT * EARLY)
            r_transpose_x(0, 0, 0, first=True)
            r_up(0, 0, first=True)
            r_transpose_x(1, 0, 1, first=True)
            r_transpose_mid(0, 0, first=True)
            r_up(1, 1, first=True)
            r_transpose_x(2, 1, 0)
            r_down(0, 0, first=True)
            r_transpose_mid(1, 1, first=True)
            with pe.Fori(1, NJ // 2 - 1) as i:
                j = 2 * i
                r_up(j, 0)
                r_transpose_x(j + 1, i, 1)
                r_down(j - 1, 1)
                r_transpose_mid(j, 0)
                r_up(j + 1, 1)
                r_transpose_x(j + 2, i + 1, 0)
                r_down(j, 0)
                r_transpose_mid(j + 1, 1)
            r_up(NJ - 2, 0)
            r_transpose_x(NJ - 1, NJ // 2 - 1, 1)
            r_down(NJ - 3, 1)
            r_transpose_mid(NJ - 2, 0)
            r_up(NJ - 1, 1)
            r_down(NJ - 2, 0)
            r_transpose_mid(NJ - 1, 1)
            r_down(NJ - 1, 1)

            shared_up(EARLY // 2, 0)
            pe.wait_ge(rrow_ready, NJ)
            with pe.Fori(EARLY // 2, A_HALF - 1) as i:
                shared_up(i, 1)
                shared_down(i, 0)
                shared_up(i + 1, 0)
                shared_down(i, 1)
            shared_up(A_HALF - 1, 1)
            shared_down(A_HALF - 1, 0)
            shared_down(A_HALF - 1, 1)


def kernel(x, itok_B_0_6, L0_cond_W, L0_cond_A, L0_cond_Bm, L0_cond_scalings, L0_ffn_Wsh_up, L0_ffn_Wsh_down,
           L0_ffn_Wrt_up, L0_ffn_Wrt_down, L0_ffn_W_router):
    import numpy as np
    import concourse.bacc as bacc
    from concourse.bass_utils import run_bass_kernel_spmd

    def blocks(w, e, k, n):
        return np.ascontiguousarray(np.asarray(w).reshape(e, k, P, n).transpose(2, 0, 1, 3))

    x = np.asarray(x)
    a = np.asarray(L0_cond_A).reshape(AR, H)
    arrays = {
        "xT": np.ascontiguousarray(x.reshape(NC, CHUNK, HK, P).transpose(0, 3, 2, 1)).reshape(NC, P, HK * CHUNK),
        "x_rows": np.ascontiguousarray(x.reshape(TOK, H)),
        "idx": np.asarray(itok_B_0_6),
        "WT": blocks(np.asarray(L0_cond_W).T, 1, HK, H)[:, 0],
        "AT": blocks(a.T, 1, HK, AR)[:, 0],
        "BmT": np.ascontiguousarray(np.asarray(L0_cond_Bm).transpose(0, 2, 1)).reshape(AR, H),
        "scal": np.repeat(np.asarray(L0_cond_scalings), RANK).reshape(AR, 1),
        "sh_up": blocks(L0_ffn_Wsh_up, E_SH, HK, D),
        "sh_dn": blocks(L0_ffn_Wsh_down, E_SH, DM, H),
        "rt_up": blocks(L0_ffn_Wrt_up, E_RT, HK, D),
        "rt_dn": blocks(L0_ffn_Wrt_down, E_RT, DM, H),
        "w_r": blocks(L0_ffn_W_router, 1, HK, E_RT)[:, 0],
    }
    arrays = {name: np.ascontiguousarray(v) for name, v in arrays.items()}
    nc = bacc.Bacc("TRN2", target_bir_lowering=False, num_devices=1)
    args = [nc.dram_tensor(name, v.shape, mybir.dt.from_np(v.dtype), kind="ExternalInput").ap()
            for name, v in arrays.items()]
    out = nc.dram_tensor("out", [TOK, H], F32, kind="ExternalOutput").ap()
    adaln_moe_kernel(nc, *args, out)
    r = run_bass_kernel_spmd(nc, [arrays], core_ids=[0])
    return r.results[0]["out"].reshape(B, S, H)
```

```python
from contextlib import ExitStack

import concourse.bass as bass
from concourse import mybir

F32 = mybir.dt.float32
BF16 = mybir.dt.bfloat16
F16 = mybir.dt.float16
I32 = mybir.dt.int32
U32 = mybir.dt.uint32
ALU = mybir.AluOpType
ACT = mybir.ActivationFunctionType
AX_X = mybir.AxisListType.X
RMAX = bass.bass_isa.ReduceOp.max

P = 128
B, S, H = 64, 64, 512
TOK = B * S
HK = H // P
D = 256
DM = D // P
E_SH, E_RT = 2, 16
K_TOP = 2
N_AD, RANK = 8, 16
AR = N_AD * RANK
assert AR == P

CHUNK = 256
NT = CHUNK // P
NB = CHUNK // S
NC = TOK // CHUNK
TT = TOK // P
EM = E_SH * DM
EARLY = 6
LATE = NC - EARLY
NJ = (TOK * K_TOP + E_RT * (P - 1)) // P
NJ += NJ % 2
GRP = 8
NG = TT // GRP * K_TOP
WU, WD = HK * D, DM * H
UP_HI, UP_LO, DN_HI, DN_LO = 0, WU, 2 * WU, 2 * WU + WD
WE = 2 * (WU + WD)
SPLITS = 2 * (E_RT + 1)
A_HALF = NC // 2
SCALED = SH_UP, SH_DN, RT_UP, RT_DN, C_EARLY, C_ALL = range(6)
SH_FIRST, SH_REST, ROUTED = range(3)
EXP_ONE = 1 << 23
TOP = 14
BIAS = 127
HEAD = 2 * (TOP + 1) + H.bit_length() - 1 - (TOP + 1)
assert EARLY == NC - EARLY - 4 and EARLY <= A_HALF and NC % 4 == 0 and NC == E_RT and EM == HK and NG == 8


def adaln_moe_kernel(nc, xT, x_rows, idx, WT, AT, BmT, scal, sh_up, sh_dn, rt_w, w_r, out):
    ctx = ExitStack()
    with ctx:
        def sb(name, shape, dt=F32):
            return ctx.enter_context(nc.sbuf_tensor(name, shape, dt))

        def sem(name):
            return ctx.enter_context(nc.semaphore(name))

        def sems(name, n=2):
            return [sem(f"{name}{s}") for s in range(n)]

        xc_dram = nc.dram_tensor("xc_dram", [TOK, H], F32, kind="Internal").ap()
        xcT_dram = nc.dram_tensor("xcT_dram", [NC, P, HK * CHUNK], F32, kind="Internal").ap()
        s_dram = nc.dram_tensor("s_dram", [TOK, H], F32, kind="Internal").ap()
        r_dram = nc.dram_tensor("r_dram", [NJ * P, H], F32, kind="Internal").ap()

        shw = sb("shw", [P, E_SH, WE], F16)
        rtw = sb("rtw", [P, E_RT + 1, WE], F16)

        def arrived(e):
            return rtw[:, bass.ds(e, 1), :].rearrange("p a n -> p (a n)").bitcast(F32)

        spare = rtw[:, E_RT, :].bitcast(F32)
        condT_in = spare[:, 0:HK * CHUNK]
        xres = spare[:, HK * CHUNK:].rearrange("p (t h) -> p t h", t=NT)
        act_in = [sb(f"act_in{s}", [P, HK, CHUNK]) for s in range(2)]
        rows = [sb(f"rows{s}", [P, NT, H]) for s in range(2)]
        hid = [sb(f"hid{s}", [P, HK, CHUNK]) for s in range(2)]
        xam = [sb(f"xam{s}", [P, CHUNK]) for s in range(2)]
        actT = [v[:].rearrange("p k t -> p (k t)").bitcast(F16).rearrange("p (a k t) -> p a k t", a=2, k=HK) for v in act_in]
        hidT = [v[:].rearrange("p k t -> p (k t)").bitcast(F16).rearrange("p (a k t) -> p a k t", a=2, k=EM) for v in hid]
        tmp = sb("tmp", [P, EM * CHUNK])
        mid = [tmp[:, s * D:(s + 1) * D] for s in range(2)]
        midT = [tmp[:, (2 + s) * D:(3 + s) * D].bitcast(F16).rearrange("p (a m t) -> p a m t", a=2, m=DM) for s in range(2)]

        region = sb("region", [P, HK * H + HK * AR + H + HK * E_RT])

        def carve(sizes):
            at, views = 0, []
            for shape, dt in sizes:
                n = 1
                for d in shape:
                    n *= d
                words = n * (4 if dt is F32 else 2) // 4
                v = region[:, at:at + words]
                at += words
                if dt is not F32:
                    v = v.bitcast(dt)
                if len(shape) == 2:
                    v = v.rearrange("p (a b) -> p a b", a=shape[0])
                if len(shape) == 3:
                    v = v.rearrange("p (a b c) -> p a b c", a=shape[0], b=shape[1])
                views.append(v)
            assert at <= HK * H + HK * AR + H + HK * E_RT
            return views

        wt, at_, bmt, wr = carve([((HK, H), F32), ((HK, AR), F32), ((H,), F32), ((HK, E_RT), F32)])
        acc0, acc1, pref = carve([((TT, E_RT), F32)] * 3)
        inv_bufs = carve([((GRP, P), F16), ((GRP, NJ), F16)] * 2)
        in_part, in_val = inv_bufs[0::2], inv_bufs[1::2]
        routed_bufs = carve([((H,), F32), ((2, HK, P), F16), ((H,), F32)] * 2)
        xg, xgT, rrow = routed_bufs[0::3], routed_bufs[1::3], routed_bufs[2::3]

        late = rtw[:].rearrange("p e n -> p (e n)").bitcast(F32)
        assert (NC + 4 * K_TOP) * NT * H <= E_RT * WE // 2

        def sum_rows(c, n=1):
            return late[:, bass.ds(c * NT * H, n * NT * H)].rearrange("p (t h) -> p t h", h=H)

        def routed_row(slot, r, t):
            at = ((NC + slot * K_TOP + r) * NT + t) * H
            return late[:, at:at + H]


        ident = sb("ident", [P, P])
        lower = sb("lower", [P, P], BF16)
        ones = sb("ones", [P, P], BF16)
        iota_p = sb("iota_p", [P, P], F16)
        iota_j = sb("iota_j", [P, NJ], F16)
        iota_e = sb("iota_e", [P, E_RT])
        tok_no = sb("tok_no", [P, TT])
        part_i = sb("part_i", [P, 1], I32)
        part_f = sb("part_f", [P, 1])
        ad_i = sb("ad_i", [P, 1], I32)
        ad_f = sb("ad_f", [P, 1])
        sc_col = sb("sc_col", [P, 1])
        idx_b = sb("idx_b", [P, B], I32)
        mask = sb("mask", [P, B])
        lg = sb("lg", [P, TT, E_RT])
        lg_c = [sb(f"lg_c{s}", [P, NT, E_RT]) for s in range(2)]
        best_c = [sb(f"best_c{s}", [P, NT, 8]) for s in range(2)]
        best_i_c = [sb(f"best_i_c{s}", [P, NT, 8], U32) for s in range(2)]
        best = sb("best", [P, TT, K_TOP])
        zsum = sb("zsum", [P, TT])
        gate = sb("gate", [P, K_TOP, TT])
        chosen = sb("chosen", [P, K_TOP, TT])
        oh = [sb(f"oh{r}", [P, TT, E_RT], BF16) for r in range(K_TOP)]
        oh_sum = sb("oh_sum", [P, TT, E_RT], BF16)
        cnt_i = sb("cnt_i", [P, E_RT], I32)
        tiles_i = sb("tiles_i", [P, E_RT], I32)
        tiles_f = sb("tiles_f", [P, E_RT])
        end_t = [sb(f"end_t{s}", [P, E_RT]) for s in range(2)]
        start_s = sb("start_s", [P, E_RT])
        pos_f = sb("pos_f", [P, K_TOP, TT])
        pos = sb("pos", [P, K_TOP, TT], I32)
        hi_i = sb("hi_i", [P, K_TOP, TT], I32)
        lo_i = sb("lo_i", [P, K_TOP, TT], I32)
        hi_f = sb("hi_f", [P, K_TOP, TT])
        lo_f = sb("lo_f", [P, K_TOP, TT])
        past = sb("past", [P, E_RT])
        tile_col = sb("tile_col", [P, 1])
        tile_e = sb("tile_e", [1, NJ // 2, 4], I32)
        tok = sb("tok", [P, NJ], I32)
        lot_max = sb("lot_max", [P, 2, E_RT])
        c_chunk = sb("c_chunk", [P, NC])
        largest = sb("largest", [P, len(SCALED)])
        largest_all = sb("largest_all", [P, len(SCALED)])
        expo = sb("expo", [P, len(SCALED)], I32)
        neg_expo = sb("neg_expo", [P, len(SCALED)], I32)
        scale = sb("scale", [P, len(SCALED)], I32)
        unscale = sb("unscale", [P, len(SCALED)], I32)
        un_up, to_mid, un_dn = sb("un_up", [P, 3]), sb("to_mid", [P, 3]), sb("un_dn", [P, 3])

        def col(v, n):
            return v[:, n:n + 1]

        slot_idx = [sb(f"slot_idx{s}", [P, 1], I32) for s in range(2)]
        row_idx = [sb(f"row_idx{s}", [P, K_TOP, NT], I32) for s in range(4)]

        bank = [ctx.enter_context(nc.psum_tensor(f"bank{i}", [P, 512], F32)) for i in range(8)]
        XA, COND, XPOSE, LOGIT = bank[0], bank[1:3], bank[3:5], bank[5]
        PRE, TOT, INV, TILE_E = bank[6], bank[7], bank[0], bank[5]
        UP, DOWN = bank[1:3], bank[3:5]
        R_XT, R_UP, R_MT, R_DN = [bank[0], bank[5]], bank[6:8], bank[1:3], bank[3:5]

        w_adapters, w_mask, w_cond, w_shared = sem("w_adapters"), sem("w_mask"), sem("w_cond"), sem("w_shared")
        w_loaded = sems("w_loaded", 4)
        lot_max_ready, largest_ready, reduced, scale_ready, un_ready = (
            sem("lot_max_ready"), sem("largest_ready"), sem("reduced"), sem("scale_ready"), sem("un_ready"))
        w_half, w_split, c_chunk_ready = sem("w_half"), sem("w_split"), sem("c_chunk_ready")
        condT_loaded, condT_half, actT_ready = sem("condT_loaded"), sem("condT_half"), sem("actT_ready")
        hid_half, hid_ready = sem("hid_half"), sem("hid_ready")
        xgT_half, midT_half = sem("xgT_half"), sem("midT_half")
        iotas, masks, consts = sem("iotas"), sem("masks"), sem("consts")
        v_step = sem("v_step")
        act_loaded, act_used = sems("act_loaded"), sem("act_used")
        xa_ready, xam_ready = sem("xa_ready"), sem("xam_ready")
        cond_ready, rows_ready = sem("cond_ready"), sem("rows_ready")
        xpose_ready, condT_ready = sem("xpose_ready"), sem("condT_ready")
        rows_stored, condT_stored = sems("rows_stored"), sems("condT_stored")
        logit_ready, logit_copied, best_ready = sem("logit_ready"), sem("logit_copied"), sem("best_ready")
        place_found, top_ready = sem("place_found"), sem("top_ready")
        onehot_ready, prefix_ready = sem("onehot_ready"), sem("prefix_ready")
        shifted_ready, exp_ready = sem("shifted_ready"), sem("exp_ready")
        tile_col_ready, tile_row_ready = sem("tile_col_ready"), sem("tile_row_ready")
        place_ready, place_used, sorted_ready = sem("place_ready"), sem("place_used"), sem("sorted_ready")
        up_ready, gelu_ready = sem("up_ready"), sem("gelu_ready")
        down_ready, shared_ready = sem("down_ready"), sem("shared_ready")
        x_loaded, sum_ready = sem("x_loaded"), sem("sum_ready")
        idx_first, idx_ready = sem("idx_first"), sem("idx_ready")
        xg_loaded = sems("xg_loaded")
        xgT_psum, xgT_ready = sem("xgT_psum"), sem("xgT_ready")
        r_up_ready, r_gelu_ready = sem("r_up_ready"), sem("r_gelu_ready")
        midT_psum, midT_ready = sem("midT_psum"), sem("midT_ready")
        r_dn_ready, rrow_ready = sem("r_dn_ready"), sem("rrow_ready")
        rrow_stored = sems("rrow_stored")
        c_idx_first, c_idx_ready, e_idx_first, e_idx_ready = (
            sem("c_idx_first"), sem("c_idx_ready"), sem("e_idx_first"), sem("e_idx_ready"))
        y_loaded, e_loaded, c_r_loaded = sems("y_loaded"), sem("e_loaded"), sems("c_r_loaded", 4)
        half_weighed, weighed, e_half_weighed, e_weighed = (
            sem("half_weighed"), sem("weighed"), sem("e_half_weighed"), sem("e_weighed"))
        out_stored, e_stored = sem("out_stored"), sem("e_stored")

        block = ctx.enter_context(nc.Block())

        def flat(ap):
            return ap.rearrange("p k t -> p (k t)")

        def chunk_rows(dram, c):
            return dram[bass.ds(c * CHUNK, CHUNK), :].rearrange("(t p) h -> p t h", p=P)

        def chunk_T(dram, c):
            return dram[bass.ds(c, 1)].rearrange("a p n -> p (a n)")

        def tile_rows(dram, n):
            return dram[bass.ds(n * P, P), :]

        def condT_of(first=False):
            return tmp[:] if first else condT_in

        def by_block(v):
            return v.rearrange("p (k t) -> p k t", k=HK)

        @block.sync
        def _(sp):
            sp.dma_start(at_, AT).then_inc(w_adapters, 16)
            sp.dma_start(flat(act_in[0][:]), chunk_T(xT, 0)).then_inc(act_loaded[0], 16)
            sp.dma_start(sc_col[:], scal).then_inc(w_mask, 16)
            sp.dma_start(idx_b[:], idx.partition_broadcast(P)).then_inc(w_mask, 16)
            for dst, src in ((wt, WT), (bmt, BmT), (wr, w_r)):
                sp.dma_start(dst, src).then_inc(w_cond, 16)
            sp.dma_start(flat(act_in[1][:]), chunk_T(xT, 1)).then_inc(act_loaded[1], 16)
            sp.dma_start(arrived(0), sh_up).then_inc(w_shared, 16)
            sp.dma_start(spare, sh_dn).then_inc(w_shared, 16)
            for r in range(4):
                sp.dma_start(arrived(r + 1), rt_w[:, r, :]).then_inc(w_loaded[r], 16)

            def cond_chunk(i, s, more):
                c = 2 * i + s
                if more:
                    sp.wait_ge(act_used, c + 1)
                    sp.dma_start(flat(act_in[s][:]), chunk_T(xT, c + 2)).then_inc(act_loaded[s], 16)
                sp.wait_ge(rows_ready, NT * c + NT)
                sp.dma_start(chunk_rows(xc_dram, c), rows[s][:]).then_inc(rows_stored[s], 16)
                sp.wait_ge(condT_ready, NT * c + NT)
                sp.dma_start(chunk_T(xcT_dram, c), flat(hid[s][:])).then_inc(condT_stored[s], 16)

            with sp.Fori(0, E_RT // 4 - 1) as i:
                for s in range(2):
                    cond_chunk(i, s, True)
                    if s:
                        sp.wait_ge(w_split, 2)
                    for r in (2 * s, 2 * s + 1):
                        n = 4 * i + r
                        sp.wait_ge(lot_max_ready, n + 1)
                        sp.dma_start(arrived(n + 5), rt_w[:, bass.ds(n + 4, 1), :].rearrange("p a n -> p (a n)")).then_inc(w_loaded[r], 16)
            with sp.Fori(E_RT // 4 - 1, A_HALF - 1) as i:
                for s in range(2):
                    cond_chunk(i, s, True)

            def load_condT(c, first=False):
                sp.dma_start(condT_of(first), chunk_T(xcT_dram, c)).then_inc(condT_loaded, 16)

            def load_x(c):
                sp.dma_start(xres, chunk_rows(x_rows, c)).then_inc(x_loaded, 16)

            sp.wait_ge(condT_stored[0], 16)
            load_condT(0, first=True)
            cond_chunk(A_HALF - 1, 0, False)
            sp.wait_ge(w_split, SPLITS)
            sp.wait_ge(condT_half, 1)
            sp.wait_ge(condT_stored[1], 16)
            load_condT(1)
            load_x(0)
            cond_chunk(A_HALF - 1, 1, False)
            for s in range(2):
                sp.wait_ge(condT_stored[s], 16 * A_HALF)

            def next_condT(c):
                sp.wait_ge(actT_ready, c + 2)
                load_condT(c + 2)

            next_condT(0)
            for c in range(EARLY):
                if c + 1 < EARLY:
                    next_condT(c + 1)
                sp.wait_ge(sum_ready, c + 1)
                sp.dma_start(chunk_rows(s_dram, c), rows[c % 2][:]).then_inc(rows_stored[c % 2], 16)
                if c + 1 < EARLY:
                    load_x(c + 1)

            with sp.Fori(0, NJ // 2) as i:
                for s in range(2):
                    j = 2 * i + s
                    sp.wait_ge(rrow_ready, j + 1)
                    sp.dma_start(tile_rows(r_dram, j), rrow[s]).then_inc(rrow_stored[s], 16)

            def load_y(c, s):
                sp.dma_start(sum_rows(c), chunk_rows(x_rows, c)).then_inc(y_loaded[s], 16)

            def late_loads(i, s):
                next_condT(2 * i + s)
                sp.wait_ge(y_loaded[s], 16 * (i - EARLY // 2 + 1))
                load_y(2 * i + s + 2, s)

            def store_sums(c):
                sp.wait_ge(shared_ready, NT * c + NT)
                sp.dma_start(chunk_rows(out, c), sum_rows(c)).then_inc(out_stored, 16)

            sp.wait_ge(r_dn_ready, NJ)
            for s in range(2):
                load_y(EARLY + s, s)
            late_loads(EARLY // 2, 0)
            for s in range(2):
                sp.wait_ge(rows_stored[s], 16 * (A_HALF + EARLY // 2))
            sp.dma_start(sum_rows(0, EARLY), s_dram[0:EARLY * CHUNK, :].rearrange("(t p) h -> p t h", p=P)).then_inc(e_loaded, 16)
            late_loads(EARLY // 2, 1)
            store_sums(EARLY)
            with sp.Fori(EARLY // 2 + 1, A_HALF - 1) as i:
                for s in range(2):
                    late_loads(i, s)
                    store_sums(2 * i + s - 1)
            sp.wait_ge(e_weighed, EARLY)
            sp.dma_start(out[0:EARLY * CHUNK, :].rearrange("(t p) h -> p t h", p=P), sum_rows(0, EARLY)).then_inc(e_stored, 16)
            for c in range(NC - 3, NC):
                store_sums(c)
            sp.wait_ge(out_stored, 16 * LATE)
            sp.wait_ge(e_stored, 16)

        @block.gpsimd
        def _(pool):
            def iota(dst, n):
                nc.gpsimd.iota(dst, [[1, n]], base=0, channel_multiplier=0,
                               allow_small_or_imprecise_dtypes=True).then_inc(iotas, 1)

            nc.gpsimd.iota(part_i[:], [[0, 1]], base=0, channel_multiplier=1).then_inc(iotas, 1)
            iota(iota_p[:], P)
            iota(iota_j[:], NJ)
            iota(iota_e[:], E_RT)
            nc.gpsimd.iota(tok_no[:], [[P, TT]], base=-TOK // 2, channel_multiplier=1,
                           allow_small_or_imprecise_dtypes=True).then_inc(iotas, 1)
            nc.gpsimd.memset(ident[:], 0.0).then_inc(masks, 1)
            nc.gpsimd.memset(ones[:], 1.0).then_inc(masks, 1)
            nc.gpsimd.memset(lower[:], 1.0).then_inc(masks, 1)
            pool.wait_ge(masks, 3)
            nc.gpsimd.affine_select(out=ident[:], in_=ident[:], compare_op=ALU.not_equal, fill=1.0, base=0,
                                    pattern=[[-1, P]], channel_multiplier=1).then_inc(consts, 1)
            nc.gpsimd.affine_select(out=lower[:], in_=lower[:], compare_op=ALU.is_gt, fill=0.0, base=0,
                                    pattern=[[1, P]], channel_multiplier=-1).then_inc(consts, 1)

            def reduce_max(n, a, b):
                pool.wait_ge(largest_ready, n)
                nc.gpsimd.partition_all_reduce(largest_all[:, a:b], largest[:, a:b], P, RMAX).then_inc(reduced, 1)

            reduce_max(1, SH_UP, RT_UP)
            reduce_max(2, RT_UP, C_ALL)

            def add_x(i, s):
                c = 2 * i + s
                pool.wait_ge(shared_ready, NT * c + NT)
                pool.wait_ge(x_loaded, 16 * (c + 1))
                nc.gpsimd.tensor_tensor(rows[s][:], rows[s][:], xres, ALU.add).then_inc(sum_ready, 1)

            def low_condT(c):
                pool.wait_ge(condT_half, c + 1)
                nc.gpsimd.tensor_tensor(actT[c % 2][:, 1], by_block(condT_of(c == 0)), actT[c % 2][:, 0],
                                        ALU.subtract).then_inc(actT_ready, 1)

            def low_hid(c):
                pool.wait_ge(hid_half, c + 1)
                nc.gpsimd.tensor_tensor(hidT[c % 2][:, 1], by_block(tmp[:]), hidT[c % 2][:, 0],
                                        ALU.subtract).then_inc(hid_ready, 1)

            low_condT(0)
            low_condT(1)
            reduce_max(3, C_ALL, C_ALL + 1)
            for c in range(EARLY - 1):
                low_hid(c)
                low_condT(c + 2)
                if c:
                    add_x((c - 1) // 2, (c - 1) % 2)

            pool.wait_ge(sorted_ready, 1)
            for s in range(2):
                pool.wait_ge(rows_stored[s], 16 * A_HALF)

            def gather(i, s, first):
                j = 2 * i + s
                copied = idx_first if first else idx_ready
                if not first:
                    pool.wait_ge(xgT_psum, j - 1)
                nc.gpsimd.tensor_copy(slot_idx[s][:], tok[:, bass.ds(j, 1)]).then_inc(copied, 1)
                pool.wait_ge(sorted_ready, 1)
                pool.wait_ge(copied, j + 1 if first else j - 1)
                nc.gpsimd.indirect_dma_start(
                    out=xg[s], out_offset=None, in_=xc_dram,
                    in_offset=bass.IndirectOffsetOnAxis(ap=slot_idx[s][:].bitcast(U32), axis=0),
                ).then_inc(xg_loaded[s], 16)

            for s in range(2):
                gather(0, s, True)
            low_hid(EARLY - 1)
            low_condT(EARLY + 1)
            add_x((EARLY - 2) // 2, (EARLY - 2) % 2)
            for s in range(2):
                gather(1, s, False)
            add_x((EARLY - 1) // 2, (EARLY - 1) % 2)
            with pool.Fori(2, NJ // 2) as i:
                for s in range(2):
                    gather(i, s, False)

            def gather_back(c, slot, n, first_copied, copied, used=None):
                if used is None:
                    copied, before = first_copied, n + 1
                else:
                    before = n - 1
                    pool.wait_ge(used, before)
                nc.gpsimd.tensor_copy(row_idx[slot][:], pos[:, :, bass.ds(c * NT, NT)]).then_inc(copied, 1)
                pool.wait_ge(sorted_ready, 1)
                pool.wait_ge(copied, before)
                for r in range(K_TOP):
                    for t in range(NT):
                        nc.gpsimd.indirect_dma_start(
                            out=routed_row(slot, r, t), out_offset=None, in_=r_dram,
                            in_offset=bass.IndirectOffsetOnAxis(ap=row_idx[slot][:, r, t:t + 1].bitcast(U32), axis=0),
                        ).then_inc(c_r_loaded[slot], 16)

            def gather_late(c, s, used=None):
                gather_back(c, s, c - EARLY, c_idx_first, c_idx_ready, used)

            def gather_early(k, s, used=None):
                gather_back(k, 2 + s, k, e_idx_first, e_idx_ready, used)

            pool.wait_ge(r_dn_ready, NJ)
            for s in range(2):
                pool.wait_ge(rrow_stored[s], 16 * (NJ // 2))
            for s in range(2):
                gather_late(EARLY + s, s)
            for s in range(2):
                gather_early(s, s)
            with pool.Fori(EARLY // 2 + 1, A_HALF - 2) as i:
                for s in range(2):
                    gather_late(2 * i + s, s, weighed)
                    gather_early(2 * i + s - EARLY, s, e_weighed)
            for c in range(NC - 4, NC):
                gather_late(c, c % 2, weighed)

        @block.scalar
        def _(act):
            def high(dst, src, n):
                nc.scalar.activation(dst, src, ACT.Copy, scale=col(scale, n).bitcast(F32)).then_inc(w_half, 1)

            def high_routed(e):
                act.wait_ge(w_split, 2 * e + 1)
                high(rtw[:, bass.ds(e, 1), UP_HI:UP_HI + WU].rearrange("p a n -> p (a n)"), arrived(e + 1)[:, 0:WU], RT_UP)
                act.wait_ge(w_split, 2 * e + 2)
                high(rtw[:, bass.ds(e, 1), DN_HI:DN_HI + WD].rearrange("p a n -> p (a n)"), arrived(e + 1)[:, WU:], RT_DN)

            def high_condT(c, s, n=C_ALL, early=False):
                act.wait_ge(condT_loaded, 16 * (c + 1))
                if early and c < 2:
                    act.wait_ge(act_used, NC - 1 + c)
                else:
                    act.wait_ge(up_ready, EM * c - EM)
                src, by = condT_of(early and c == 0), col(scale, n).bitcast(F32)
                last = nc.scalar.activation(actT[s][:, 0], by_block(src), ACT.Copy, scale=by)
                if early:
                    last = nc.scalar.activation(src, src, ACT.Copy, scale=by)
                last.then_inc(condT_half, 1)

            def cond_rows(i, s, first=False):
                c = 2 * i + s
                if not first:
                    act.wait_ge(rows_stored[s], 16 * i)
                    act.wait_ge(c_chunk_ready, c - 1)
                for t in range(NT):
                    act.wait_ge(cond_ready, NT * c + t + 1)
                    nc.scalar.copy(rows[s][:, t, :], COND[t][:]).then_inc(rows_ready, 1)

            for s in range(2):
                cond_rows(0, s, first=True)
            act.wait_ge(scale_ready, 1)
            high(shw[:, :, UP_HI:UP_HI + WU], arrived(0).rearrange("p (e n) -> p e n", e=E_SH), SH_UP)
            high(shw[:, :, DN_HI:DN_HI + WD], spare.rearrange("p (e n) -> p e n", e=E_SH), SH_DN)
            with act.Fori(1, A_HALF // 2) as i:
                for s in range(2):
                    cond_rows(i, s)
            act.wait_ge(scale_ready, 2)
            with act.Fori(A_HALF // 2, A_HALF - 1) as i:
                for s in range(2):
                    for n in range(2):
                        high_routed(4 * i - NC + 2 * s + n)
                    cond_rows(i, s)
            for s in range(2):
                for n in range(2):
                    high_routed(E_RT - 4 + 2 * s + n)
                if s:
                    high_condT(0, 0, C_EARLY, early=True)
                cond_rows(A_HALF - 1, s)

            def gelus(c, s, n=SH_REST, early=False):
                if early and c == 0:
                    act.wait_ge(actT_ready, 1)
                else:
                    act.wait_ge(hid_ready, c)
                for em in range(EM):
                    act.wait_ge(up_ready, EM * c + em + 1)
                    nc.scalar.activation(tmp[:, em * CHUNK:(em + 1) * CHUNK], UP[em % 2][:, 0:CHUNK], ACT.Gelu,
                                         scale=col(un_up, n)).then_inc(gelu_ready, 1)
                if early and c < 2:
                    act.wait_ge(condT_stored[s], 16 * A_HALF)
                else:
                    act.wait_ge(down_ready, NT * c - NT)
                act.wait_ge(gelu_ready, EM * c + EM)
                last = nc.scalar.activation(hidT[s][:, 0], by_block(tmp[:]), ACT.Copy, scale=col(to_mid, n))
                if early:
                    last = nc.scalar.activation(tmp[:], tmp[:], ACT.Copy, scale=col(to_mid, n))
                last.then_inc(hid_half, 1)

            def shared_rows(c):
                i, s, n = c // 2, c % 2, SH_FIRST
                act.wait_ge(rows_stored[s], 16 * (A_HALF + i))
                for t in range(NT):
                    act.wait_ge(down_ready, NT * c + t + 1)
                    nc.scalar.activation(rows[s][:, t, :], DOWN[t][:], ACT.Copy, scale=col(un_dn, n)).then_inc(shared_ready, 1)

            act.wait_ge(un_ready, 1)
            high_condT(1, 1, C_EARLY, early=True)
            act.wait_ge(c_chunk_ready, NC)
            for c in range(EARLY):
                gelus(c, c % 2, SH_FIRST, early=True)
                if c + 2 == EARLY:
                    act.wait_ge(scale_ready, 3)
                high_condT(c + 2, c % 2, C_EARLY if c + 2 < EARLY else C_ALL, early=True)
                if c:
                    shared_rows(c - 1)
                if c == 2:
                    act.wait_ge(shifted_ready, 1)
                    nc.scalar.activation(lg[:], lg[:], ACT.Exp)
                    nc.scalar.activation(best[:, :, 1:2], best[:, :, 1:2], ACT.Exp).then_inc(exp_ready, 1)
            act.wait_ge(un_ready, 3)

            def r_gelu(j, s):
                act.wait_ge(r_up_ready, j + 1)
                nc.scalar.activation(mid[s], R_UP[s][:, 0:D], ACT.Gelu, scale=col(un_up, ROUTED)).then_inc(r_gelu_ready, 1)

            def r_high(j, s):
                act.wait_ge(xgT_psum, j + 1)
                nc.scalar.activation(xgT[s][:, 0], R_XT[s][:].rearrange("p (k t) -> p k t", k=HK), ACT.Copy,
                                     scale=col(scale, C_ALL).bitcast(F32)).then_inc(xgT_half, 1)

            def r_rows(j, i, s, first=False):
                if not first:
                    act.wait_ge(rrow_stored[s], 16 * i)
                act.wait_ge(r_dn_ready, j + 1)
                nc.scalar.activation(rrow[s], R_DN[s][:], ACT.Copy, scale=col(un_dn, ROUTED)).then_inc(rrow_ready, 1)

            def r_step(j, i, s, first=False):
                r_gelu(j, s)
                r_high(j + 2, s)
                if not (first and j == 0):
                    r_rows(j - 1, i - 1 + s, 1 - s, first and j < 3)

            for s in range(2):
                r_high(s, s)
            shared_rows(EARLY - 1)
            for j in range(4):
                r_step(j, j // 2, j % 2, first=True)
            with act.Fori(2, NJ // 2 - 1) as i:
                for s in range(2):
                    r_step(2 * i + s, i, s)
            for j in range(NJ - 2, NJ):
                r_gelu(j, j % 2)
                r_rows(j - 1, (j - 1) // 2, (j - 1) % 2)
            r_rows(NJ - 1, NJ // 2 - 1, 1)

            def late_step(c, s):
                high_condT(c + 2, s)
                gelus(c + 1, 1 - s)

            gelus(EARLY, 0)
            for s in range(2):
                late_step(EARLY + s, s)
            with act.Fori(EARLY // 2 + 1, A_HALF - 1) as i:
                for s in range(2):
                    late_step(2 * i + s, s)
            gelus(NC - 1, 1)

        @block.vector
        def _(dve):
            steps = [0]

            def link(ins):
                steps[0] += 1
                ins.then_inc(v_step, 1)
                dve.wait_ge(v_step, steps[0])

            dve.wait_ge(w_mask, 2 * 16)
            dve.wait_ge(iotas, 5)
            link(nc.vector.tensor_scalar(ad_i[:], part_i[:], RANK.bit_length() - 1, None, ALU.logical_shift_right))
            link(nc.vector.tensor_copy(ad_f[:], ad_i[:]))
            link(nc.vector.tensor_copy(part_f[:], part_i[:]))
            link(nc.vector.tensor_scalar(mask[:], idx_b[:], ad_f[:], sc_col[:], ALU.is_equal, ALU.mult))

            def mask_xa(c, s):
                dve.wait_ge(xa_ready, c + 1)
                nc.vector.tensor_tensor(
                    xam[s][:].rearrange("p (b t) -> p b t", b=NB), XA[:, 0:CHUNK].rearrange("p (b t) -> p b t", b=NB),
                    mask[:, bass.ds(c * NB, NB)].unsqueeze(2).to_broadcast([P, NB, S]), ALU.mult,
                ).then_inc(xam_ready, 1)

            def cond_T(c, i, s, first=False):
                if not first:
                    dve.wait_ge(condT_stored[s], 16 * i)
                for t in range(NT):
                    dve.wait_ge(xpose_ready, NT * c + t + 1)
                    nc.vector.tensor_copy(hid[s][:, :, t * P:(t + 1) * P],
                                          XPOSE[t][:].rearrange("p (k t) -> p k t", k=HK)).then_inc(condT_ready, 1)

            def top(c, s):
                dve.wait_ge(logit_ready, c + 1)
                nc.vector.tensor_copy(lg_c[s][:], LOGIT[:, 0:NT * E_RT].rearrange("p (t e) -> p t e", t=NT)).then_inc(logit_copied, 1)
                dve.wait_ge(logit_copied, c + 1)
                nc.vector.tensor_copy(lg[:, bass.ds(c * NT, NT), :], lg_c[s][:])
                for t in range(NT):
                    nc.vector.max(best_c[s][:, t, :], lg_c[s][:, t, :]).then_inc(best_ready, 1)
                dve.wait_ge(best_ready, c * NT + NT)
                nc.vector.tensor_copy(best[:, bass.ds(c * NT, NT), :], best_c[s][:, :, 0:K_TOP])
                for t in range(NT):
                    nc.vector.max_index(best_i_c[s][:, t, :], best_c[s][:, t, :], lg_c[s][:, t, :]).then_inc(place_found, 1)
                dve.wait_ge(place_found, c * NT + NT)
                nc.vector.tensor_copy(chosen[:, :, bass.ds(c * NT, NT)],
                                      best_i_c[s][:, :, 0:K_TOP].rearrange("p t r -> p r t")).then_inc(top_ready, 1)

            def row_max(c, s):
                dve.wait_ge(rows_ready, NT * c + NT)
                nc.vector.tensor_reduce(c_chunk[:, bass.ds(c, 1)], rows[s][:].rearrange("p t h -> p (t h)"), AX_X, ALU.max,
                                        apply_absolute_value=True).then_inc(c_chunk_ready, 1)

            def lot_maxima(i, s):
                for r in (2 * s, 2 * s + 1):
                    e = 4 * i + r
                    dve.wait_ge(w_loaded[r], 16 * (i + 1))
                    nc.vector.tensor_reduce(lot_max[:, :, bass.ds(e, 1)].rearrange("p u a -> p (u a)"),
                                            arrived(e + 1).rearrange("p (u n) -> p u n", u=2), AX_X, ALU.max,
                                            apply_absolute_value=True).then_inc(lot_max_ready, 1)

            def scales(n, a, b):
                dve.wait_ge(reduced, n)
                link(nc.vector.tensor_scalar(expo[:, a:b], largest_all[:, a:b].bitcast(I32), 255 * EXP_ONE, None, ALU.bitwise_and))
                link(nc.vector.tensor_scalar(neg_expo[:, a:b], expo[:, a:b], float(30 * EXP_ONE), -1.0, ALU.max, ALU.mult))
                link(nc.vector.tensor_scalar(unscale[:, a:b], neg_expo[:, a:b], -1.0, float(-TOP * EXP_ONE), ALU.mult, ALU.add))
                nc.vector.tensor_scalar(scale[:, a:b], neg_expo[:, a:b], float((TOP + 2 * BIAS) * EXP_ONE), None,
                                        ALU.add).then_inc(scale_ready, 1)

            def result_scales(n, c, up, dn):
                link(nc.vector.tensor_tensor(col(un_up, n), col(unscale, c).bitcast(F32), col(unscale, up).bitcast(F32), ALU.mult))
                nc.vector.tensor_scalar(col(to_mid, n).bitcast(I32), col(un_up, n).bitcast(I32), -1.0,
                                        float((2 * BIAS - HEAD) * EXP_ONE), ALU.mult, ALU.add)
                nc.vector.scalar_tensor_tensor(col(un_dn, n), col(un_up, n), float(1 << HEAD), col(unscale, dn).bitcast(F32),
                                               ALU.mult, ALU.mult).then_inc(un_ready, 1)

            def low(dst, src, n, hi, half):
                dve.wait_ge(w_half, half)
                nc.vector.scalar_tensor_tensor(dst, src, col(scale, n).bitcast(F32), hi, ALU.mult, ALU.subtract).then_inc(w_split, 1)

            def low_routed(e):
                def part(at):
                    return rtw[:, bass.ds(e, 1), at:at + WU].rearrange("p a n -> p (a n)")

                low(part(UP_LO), arrived(e + 1)[:, 0:WU], RT_UP, part(UP_HI), 2 * e + 3)
                low(part(DN_LO), arrived(e + 1)[:, WU:], RT_DN, part(DN_HI), 2 * e + 4)

            def end_chunk(c, i, s, first=False):
                cond_T(c, i, s, first)
                top(c, s)

            def search_step(i, s, first=False):
                mask_xa(2 * i + s, s)
                row_max(2 * i + s - 1, 1 - s)
                lot_maxima(i, s)
                end_chunk(2 * i + s - 1, i - 1 + s, 1 - s, first)

            mask_xa(0, 0)
            dve.wait_ge(w_shared, 2 * 16)
            nc.vector.tensor_reduce(col(largest, SH_UP), arrived(0), AX_X, ALU.max, apply_absolute_value=True)
            nc.vector.tensor_reduce(col(largest, SH_DN), spare, AX_X, ALU.max,
                                    apply_absolute_value=True).then_inc(largest_ready, 1)
            lot_maxima(0, 0)
            search_step(0, 1, first=True)
            scales(1, SH_UP, RT_UP)
            low(shw[:, :, UP_LO:UP_LO + WU], arrived(0).rearrange("p (e n) -> p e n", e=E_SH), SH_UP, shw[:, :, UP_HI:UP_HI + WU], 1)
            low(shw[:, :, DN_LO:DN_LO + WD], spare.rearrange("p (e n) -> p e n", e=E_SH), SH_DN, shw[:, :, DN_HI:DN_HI + WD], 2)
            search_step(1, 0, first=True)
            search_step(1, 1)
            with dve.Fori(2, A_HALF // 2) as i:
                for s in range(2):
                    search_step(i, s)
            dve.wait_ge(c_chunk_ready, EARLY)
            dve.wait_ge(lot_max_ready, E_RT)
            nc.vector.tensor_reduce(largest[:, RT_UP:RT_DN + 1], lot_max[:], AX_X, ALU.max)
            nc.vector.tensor_reduce(col(largest, C_EARLY), c_chunk[:, 0:EARLY], AX_X, ALU.max).then_inc(largest_ready, 1)
            scales(2, RT_UP, C_ALL)
            result_scales(SH_FIRST, C_EARLY, SH_UP, SH_DN)
            with dve.Fori(A_HALF // 2, A_HALF) as i:
                for s in range(2):
                    c = 2 * i + s
                    mask_xa(c, s)
                    row_max(c - 1, 1 - s)
                    for n in range(2):
                        low_routed(2 * c - NC + n)
                    end_chunk(c - 1, i - 1 + s, 1 - s)
            cond_T(NC - 1, A_HALF - 1, 1)
            top(NC - 1, 1)
            dve.wait_ge(top_ready, NC)

            for r in range(K_TOP):
                link(nc.vector.tensor_tensor(oh[r][:], iota_e[:].unsqueeze(1).to_broadcast([P, TT, E_RT]),
                                             chosen[:, r, :].unsqueeze(2).to_broadcast([P, TT, E_RT]), ALU.is_equal))
            nc.vector.tensor_tensor(oh_sum[:], oh[0][:], oh[1][:], ALU.add).then_inc(onehot_ready, 1)

            row_max(NC - 1, 1)
            dve.wait_ge(c_chunk_ready, NC)
            nc.vector.tensor_reduce(col(largest, C_ALL), c_chunk[:], AX_X, ALU.max).then_inc(largest_ready, 1)

            link(nc.vector.tensor_tensor(lg[:], lg[:], best[:, :, 0:1].to_broadcast([P, TT, E_RT]), ALU.subtract))
            nc.vector.tensor_tensor(best[:, :, 1:2], best[:, :, 1:2], best[:, :, 0:1], ALU.subtract).then_inc(shifted_ready, 1)

            dve.wait_ge(prefix_ready, 1)
            link(nc.vector.tensor_copy(acc0, TOT[:].rearrange("p (t e) -> p t e", t=TT)))
            src, dst, d = acc0, acc1, 1
            while d < TT:
                nc.vector.tensor_copy(dst[:, 0:d, :], src[:, 0:d, :])
                link(nc.vector.tensor_tensor(dst[:, d:, :], src[:, d:, :], src[:, :TT - d, :], ALU.add))
                src, dst, d = dst, src, 2 * d
            link(nc.vector.tensor_scalar(cnt_i[:], src[:, TT - 1, :], float(P - 1), None, ALU.add))
            link(nc.vector.tensor_scalar(tiles_i[:], cnt_i[:], P.bit_length() - 1, None, ALU.logical_shift_right))
            link(nc.vector.tensor_copy(tiles_f[:], tiles_i[:]))
            link(nc.vector.tensor_copy(end_t[0][:], tiles_f[:]))
            a, b, d = end_t[0], end_t[1], 1
            while d < E_RT:
                nc.vector.tensor_copy(b[:, 0:d], a[:, 0:d])
                link(nc.vector.tensor_tensor(b[:, d:], a[:, d:], a[:, :E_RT - d], ALU.add))
                a, b, d = b, a, 2 * d
            link(nc.vector.tensor_tensor(start_s[:], a[:], tiles_f[:], ALU.subtract))
            link(nc.vector.tensor_scalar(start_s[:], start_s[:], float(P), None, ALU.mult))
            link(nc.vector.tensor_scalar(past[:], a[:], part_f[:], None, ALU.is_le))
            link(nc.vector.tensor_reduce(tile_col[:], past[:], AX_X, ALU.add))
            nc.vector.tensor_scalar(tile_col[:], tile_col[:], float(E_RT - 1), None, ALU.min).then_inc(tile_col_ready, 1)
            link(nc.vector.tensor_tensor(dst, src, TOT[:].rearrange("p (t e) -> p t e", t=TT), ALU.subtract))
            link(nc.vector.tensor_tensor(pref, dst, PRE[:].rearrange("p (t e) -> p t e", t=TT), ALU.add))
            link(nc.vector.tensor_tensor(pref, pref, start_s[:].unsqueeze(1).to_broadcast([P, TT, E_RT]), ALU.add))
            for r in range(K_TOP):
                link(nc.vector.tensor_tensor(acc0, oh[r][:], pref, ALU.mult))
                link(nc.vector.tensor_reduce(pos_f[:, r, :], acc0, AX_X, ALU.add))
            link(nc.vector.tensor_copy(pos[:], pos_f[:]))
            link(nc.vector.tensor_scalar(hi_i[:], pos[:], P.bit_length() - 1, None, ALU.logical_shift_right))
            link(nc.vector.tensor_scalar(lo_i[:], pos[:], P - 1, None, ALU.bitwise_and))
            link(nc.vector.tensor_copy(hi_f[:], hi_i[:]))
            link(nc.vector.tensor_copy(lo_f[:], lo_i[:]))

            scales(3, C_ALL, C_ALL + 1)
            result_scales(SH_REST, C_ALL, SH_UP, SH_DN)
            result_scales(ROUTED, C_ALL, RT_UP, RT_DN)

            def places(i, first=False):
                for s in range(2):
                    if not first:
                        dve.wait_ge(place_used, 2 * i + s - 1)
                    for n in range(GRP):
                        at = bass.ds(i * GRP + n, 1)
                        nc.vector.tensor_scalar(in_part[s][:, n, :], iota_p[:], lo_f[:, s, at], None, ALU.is_equal)
                        last = nc.vector.tensor_scalar(in_val[s][:, n, :], iota_j[:], hi_f[:, s, at], tok_no[:, at],
                                                       ALU.is_equal, ALU.mult)
                    last.then_inc(place_ready, 1)

            places(0, first=True)
            with dve.Fori(1, NG // 2) as i:
                places(i)
            dve.wait_ge(tile_row_ready, 1)
            for n in (0, 2):
                nc.vector.tensor_copy(tile_e[:, :, n:n + 2], TILE_E[0:1, n:n + NJ].rearrange("p (i m) -> p i m", m=2))
            dve.wait_ge(place_used, NG)
            nc.vector.tensor_scalar(tok[:], INV[:, 0:NJ], float(TOK // 2), None, ALU.add).then_inc(sorted_ready, 1)

            def low_xgT(j, s):
                dve.wait_ge(xgT_half, j + 1)
                nc.vector.scalar_tensor_tensor(xgT[s][:, 1], R_XT[s][:].rearrange("p (k t) -> p k t", k=HK),
                                               col(scale, C_ALL).bitcast(F32), xgT[s][:, 0], ALU.mult, ALU.subtract).then_inc(xgT_ready, 1)

            def split_midT(j, s):
                dve.wait_ge(midT_psum, j + 1)
                src = R_MT[s][:, 0:D].rearrange("p (m t) -> p m t", m=DM)
                nc.vector.tensor_scalar(midT[s][:, 0], src, col(to_mid, ROUTED), None, ALU.mult).then_inc(midT_half, 1)
                dve.wait_ge(midT_half, j + 1)
                nc.vector.scalar_tensor_tensor(midT[s][:, 1], src, col(to_mid, ROUTED), midT[s][:, 0],
                                               ALU.mult, ALU.subtract).then_inc(midT_ready, 1)

            for s in range(2):
                low_xgT(s, s)
            with dve.Fori(0, NJ // 2 - 1) as i:
                for s in range(2):
                    low_xgT(2 * i + s + 2, s)
                    split_midT(2 * i + s, s)
            for s in range(2):
                split_midT(NJ - 2 + s, s)

            dve.wait_ge(exp_ready, 1)
            link(nc.vector.tensor_reduce(zsum[:], lg[:], AX_X, ALU.add))
            link(nc.vector.reciprocal(gate[:, 0, :], zsum[:]))
            link(nc.vector.tensor_tensor(gate[:, 1, :], gate[:, 0, :], best[:, :, 1], ALU.mult))

            def low_condT(c, s):
                dve.wait_ge(condT_half, c + 1)
                nc.vector.scalar_tensor_tensor(actT[s][:, 1], by_block(condT_in), col(scale, C_ALL).bitcast(F32),
                                               actT[s][:, 0], ALU.mult, ALU.subtract).then_inc(actT_ready, 1)

            def low_hid(c, s):
                dve.wait_ge(hid_half, c + 1)
                nc.vector.scalar_tensor_tensor(hidT[s][:, 1], by_block(tmp[:]), col(to_mid, SH_REST),
                                               hidT[s][:, 0], ALU.mult, ALU.subtract).then_inc(hid_ready, 1)

            def add_routed(c, r, slot, signal):
                for t in range(NT):
                    y = sum_rows(c)[:, t, :]
                    last = nc.vector.scalar_tensor_tensor(y, routed_row(slot, r, t), gate[:, r, bass.ds(c * NT + t, 1)], y,
                                                          ALU.mult, ALU.add)
                last.then_inc(signal, 1)

            def weigh(c, slot, m, n, half, done):
                dve.wait_ge(c_r_loaded[slot], K_TOP * NT * 16 * m)
                add_routed(c, 0, slot, half)
                dve.wait_ge(half, n)
                add_routed(c, 1, slot, done)

            def weigh_late(i, s):
                m = i - EARLY // 2 + 1
                dve.wait_ge(y_loaded[s], 16 * m)
                weigh(2 * i + s, s, m, 2 * i + s - EARLY + 1, half_weighed, weighed)

            def add_shared(c):
                dve.wait_ge(weighed, c - EARLY + 1)
                for t in range(NT):
                    dve.wait_ge(down_ready, NT * c + t + 1)
                    y = sum_rows(c)[:, t, :]
                    nc.vector.scalar_tensor_tensor(y, DOWN[t][:], col(un_dn, SH_REST), y, ALU.mult, ALU.add).then_inc(shared_ready, 1)

            low_hid(EARLY, 0)
            for s in range(2):
                if s:
                    add_shared(EARLY)
                low_condT(EARLY + s + 2, s)
                low_hid(EARLY + s + 1, 1 - s)
                weigh_late(EARLY // 2, s)
            with dve.Fori(EARLY // 2 + 1, A_HALF - 1) as i:
                for s in range(2):
                    c = 2 * i + s
                    add_shared(c - 1)
                    low_condT(c + 2, s)
                    dve.wait_ge(e_loaded, 16)
                    weigh(c - EARLY - 2, 2 + s, i - EARLY // 2, c - EARLY - 1, e_half_weighed, e_weighed)
                    low_hid(c + 1, 1 - s)
                    weigh_late(i, s)
            add_shared(NC - 3)
            low_hid(NC - 1, 1)
            weigh_late(A_HALF - 1, 0)
            add_shared(NC - 2)
            weigh_late(A_HALF - 1, 1)
            add_shared(NC - 1)

        @block.tensor
        def _(pe):
            mm = nc.tensor.matmul

            def cond_products(c, i, s, first=False):
                pe.wait_ge(act_loaded[s], 16 * (i + 1))
                if not first:
                    pe.wait_ge(xam_ready, c)
                for k in range(HK):
                    last = mm(XA[:, 0:CHUNK], at_[:, k, :], act_in[s][:, k, :], start=(k == 0), stop=(k == HK - 1))
                last.then_inc(xa_ready, 1)
                if first:
                    pe.wait_ge(w_cond, 3 * 16)
                for t in range(NT):
                    if not first:
                        pe.wait_ge(rows_ready, NT * c - NT + t + 1)
                    for k in range(HK):
                        last = mm(COND[t][:], act_in[s][:, k, t * P:(t + 1) * P], wt[:, k, :], start=(k == 0), stop=False)
                last.then_inc(act_used, 1)

            def adapter_products(c, s):
                pe.wait_ge(xam_ready, c + 1)
                for t in range(NT):
                    mm(COND[t][:], xam[s][:, t * P:(t + 1) * P], bmt, start=False, stop=True).then_inc(cond_ready, 1)

            def cond_transposes(c, s, first=False):
                for t in range(NT):
                    pe.wait_ge(rows_ready, NT * c + t + 1)
                    if not first:
                        pe.wait_ge(condT_ready, NT * c - NT + t + 1)
                    for k in range(HK):
                        last = nc.tensor.transpose(XPOSE[t][:, k * P:(k + 1) * P], rows[s][:, t, k * P:(k + 1) * P], ident[:])
                    last.then_inc(xpose_ready, 1)

            def router_products(c, s, first=False):
                pe.wait_ge(condT_ready, NT * c + NT)
                if not first:
                    pe.wait_ge(logit_copied, c)
                for t in range(NT):
                    for k in range(HK):
                        last = mm(LOGIT[:, t * E_RT:(t + 1) * E_RT], hid[s][:, k, t * P:(t + 1) * P], wr[:, k, :],
                                  start=(k == 0), stop=(k == HK - 1))
                last.then_inc(logit_ready, 1)

            def cond_step(c, i, s, first=False):
                cond_products(c, i, s)
                cond_transposes(c - 1, 1 - s, first)
                adapter_products(c, s)
                router_products(c - 1, 1 - s, first)

            pe.wait_ge(w_adapters, 16)
            pe.wait_ge(consts, 2)
            cond_products(0, 0, 0, first=True)
            adapter_products(0, 0)
            cond_step(1, 0, 1, first=True)
            with pe.Fori(1, A_HALF) as i:
                cond_step(2 * i, i, 0)
                cond_step(2 * i + 1, i, 1)
            cond_transposes(NC - 1, 1)
            router_products(NC - 1, 1)

            PASSES = ((0, 0), (0, 1), (1, 0))

            def prefix_products():
                pe.wait_ge(onehot_ready, 1)
                mm(PRE[:], lower[:], oh_sum[:].rearrange("p t e -> p (t e)"), start=True, stop=True)
                mm(TOT[:], ones[:], oh_sum[:].rearrange("p t e -> p (t e)"), start=True, stop=True).then_inc(prefix_ready, 1)

            def tile_expert_product():
                pe.wait_ge(tile_col_ready, 1)
                mm(TILE_E[0:1, 0:NJ + 2], tile_col[:], ident[:, 0:NJ + 2], start=True, stop=True).then_inc(tile_row_ready, 1)

            def inversion_products(g):
                pe.wait_ge(place_ready, g + 1)
                for n in range(GRP):
                    last = mm(INV[:, 0:NJ], in_part[g % 2][:, n, :], in_val[g % 2][:, n, :],
                              start=(g == 0 and n == 0), stop=(g == NG - 1 and n == GRP - 1))
                last.then_inc(place_used, 1)

            def shared_up(i, s, first=False):
                c = 2 * i + s
                pe.wait_ge(actT_ready, c + 1)
                for em in range(EM):
                    e, m = em // DM, em % DM
                    if not (first and em < 2):
                        pe.wait_ge(gelu_ready, EM * c + em - 1)
                    for k in range(HK):
                        for n, (wp, xp) in enumerate(PASSES):
                            w0 = (UP_HI, UP_LO)[wp] + k * D + m * P
                            last = mm(UP[em % 2][:, 0:CHUNK], shw[:, e, w0:w0 + P], actT[s][:, xp, k, :],
                                      start=(k == 0 and n == 0), stop=(k == HK - 1 and n == 2))
                    last.then_inc(up_ready, 1)

            def shared_down(i, s, first=False):
                c = 2 * i + s
                pe.wait_ge(hid_ready, c + 1)
                for t in range(NT):
                    if not first:
                        pe.wait_ge(shared_ready, NT * c - NT + t + 1)
                    for em in range(EM):
                        for n, (xp, wp) in enumerate(PASSES):
                            w0 = (DN_HI, DN_LO)[wp] + em % DM * H
                            last = mm(DOWN[t][:], hidT[s][:, xp, em, t * P:(t + 1) * P], shw[:, em // DM, w0:w0 + H],
                                      start=(em == 0 and n == 0), stop=(em == EM - 1 and n == 2))
                    last.then_inc(down_ready, 1)

            pe.wait_ge(w_split, 2)
            pe.wait_ge(rows_ready, TT)
            shared_up(0, 0, first=True)
            prefix_products()
            shared_up(0, 1)
            shared_down(0, 0, first=True)
            tile_expert_product()
            shared_up(1, 0)
            inversion_products(0)
            inversion_products(1)
            shared_down(0, 1)
            inversion_products(2)
            inversion_products(3)
            shared_up(1, 1)
            inversion_products(4)
            inversion_products(5)
            shared_down(1, 0)
            inversion_products(6)
            inversion_products(7)
            shared_up(2, 0)
            shared_down(1, 1)
            shared_up(2, 1)
            shared_down(2, 0)

            def r_transpose_x(j, i, s, first=False):
                pe.wait_ge(xg_loaded[s], 16 * (i + 1))
                if not first:
                    pe.wait_ge(xgT_ready, j - 1)
                for k in range(HK):
                    last = nc.tensor.transpose(R_XT[s][:, k * P:(k + 1) * P], xg[s][:, k * P:(k + 1) * P], ident[:])
                last.then_inc(xgT_psum, 1)

            def r_experts(i):
                return nc.values_load_multi_w_load_instructions(
                    tile_e[0:1, bass.ds(i, 1), 0:3].rearrange("p a m -> p (a m)"), engines=(mybir.EngineType.PE,), min_val=0, max_val=E_RT - 1,
                    skip_runtime_bounds_check_because="a count of experts, cut off at the last one by the vector engine")[1]

            def r_up(j, s, e, first=False):
                pe.wait_ge(xgT_ready, j + 1)
                if not first:
                    pe.wait_ge(r_gelu_ready, j - 1)
                for k in range(HK):
                    for n, (xp, wp) in enumerate(PASSES):
                        w0 = (UP_HI, UP_LO)[wp] + k * D
                        last = mm(R_UP[s][:, 0:D], xgT[s][:, xp, k, :], rtw[:, bass.ds(e, 1), w0:w0 + D].rearrange("p a d -> p (a d)"),
                                  start=(k == 0 and n == 0), stop=(k == HK - 1 and n == 2))
                last.then_inc(r_up_ready, 1)

            def r_transpose_mid(j, s, first=False):
                pe.wait_ge(r_gelu_ready, j + 1)
                if not first:
                    pe.wait_ge(midT_ready, j - 1)
                for m in range(DM):
                    last = nc.tensor.transpose(R_MT[s][:, m * P:(m + 1) * P], mid[s][:, m * P:(m + 1) * P], ident[:])
                last.then_inc(midT_psum, 1)

            def r_down(j, s, e, first=False):
                pe.wait_ge(midT_ready, j + 1)
                if not first:
                    pe.wait_ge(rrow_ready, j - 1)
                for m in range(DM):
                    for n, (xp, wp) in enumerate(PASSES):
                        w0 = (DN_HI, DN_LO)[wp] + m * H
                        last = mm(R_DN[s][:], midT[s][:, xp, m, :], rtw[:, bass.ds(e, 1), w0:w0 + H].rearrange("p a h -> p (a h)"),
                                  start=(m == 0 and n == 0), stop=(m == DM - 1 and n == 2))
                last.then_inc(r_dn_ready, 1)

            pe.wait_ge(w_split, SPLITS)
            pe.wait_ge(sorted_ready, 1)
            pe.wait_ge(gelu_ready, EM * EARLY)
            def r_pair(i, first=False, more=2):
                e = r_experts(i)
                for s in range(2):
                    j = 2 * i + s
                    r_transpose_mid(j, s, first and i == 0)
                    if s == 0 or more:
                        r_up(j + 1, 1 - s, e[s + 1], first and i == 0 and s == 0)
                    if more > s:
                        r_transpose_x(j + 3, i + 1 + s, 1 - s)
                    if first and i == 0 and s == 0:
                        pe.wait_ge(shared_ready, NT * EARLY)
                    r_down(j, s, e[s], first and i == 0)

            for s in range(2):
                r_transpose_x(s, 0, s, first=True)
            shared_down(2, 1)
            r_up(0, 0, r_experts(0)[0], first=True)
            r_transpose_x(2, 1, 0)
            for i in range(2):
                r_pair(i, first=True)
            with pe.Fori(2, NJ // 2 - 2) as i:
                r_pair(i)
            r_pair(NJ // 2 - 2, more=1)
            r_pair(NJ // 2 - 1, more=0)

            shared_up(EARLY // 2, 0)
            pe.wait_ge(rrow_ready, NJ)
            with pe.Fori(EARLY // 2, A_HALF - 1) as i:
                shared_up(i, 1)
                shared_down(i, 0)
                shared_up(i + 1, 0)
                shared_down(i, 1)
            shared_up(A_HALF - 1, 1)
            shared_down(A_HALF - 1, 0)
            shared_down(A_HALF - 1, 1)


def kernel(x, itok_B_0_6, L0_cond_W, L0_cond_A, L0_cond_Bm, L0_cond_scalings, L0_ffn_Wsh_up, L0_ffn_Wsh_down,
           L0_ffn_Wrt_up, L0_ffn_Wrt_down, L0_ffn_W_router):
    import numpy as np
    import concourse.bacc as bacc
    from concourse.bass_utils import run_bass_kernel_spmd

    def blocks(w, e, k, n):
        return np.ascontiguousarray(np.asarray(w).reshape(e, k, P, n).transpose(2, 0, 1, 3))

    x = np.asarray(x)
    a = np.asarray(L0_cond_A).reshape(AR, H)
    arrays = {
        "xT": np.ascontiguousarray(x.reshape(NC, CHUNK, HK, P).transpose(0, 3, 2, 1)).reshape(NC, P, HK * CHUNK),
        "x_rows": np.ascontiguousarray(x.reshape(TOK, H)),
        "idx": np.asarray(itok_B_0_6),
        "WT": blocks(np.asarray(L0_cond_W).T, 1, HK, H)[:, 0],
        "AT": blocks(a.T, 1, HK, AR)[:, 0],
        "BmT": np.ascontiguousarray(np.asarray(L0_cond_Bm).transpose(0, 2, 1)).reshape(AR, H),
        "scal": np.repeat(np.asarray(L0_cond_scalings), RANK).reshape(AR, 1),
        "sh_up": blocks(L0_ffn_Wsh_up, E_SH, HK, D).reshape(P, E_SH * WU),
        "sh_dn": blocks(L0_ffn_Wsh_down, E_SH, DM, H).reshape(P, E_SH * WD),
        "rt_w": np.concatenate([blocks(L0_ffn_Wrt_up, E_RT, HK, D).reshape(P, E_RT, WU),
                                blocks(L0_ffn_Wrt_down, E_RT, DM, H).reshape(P, E_RT, WD)], axis=2),
        "w_r": blocks(L0_ffn_W_router, 1, HK, E_RT)[:, 0],
    }
    arrays = {name: np.ascontiguousarray(v) for name, v in arrays.items()}
    nc = bacc.Bacc("TRN2", target_bir_lowering=False, num_devices=1)
    args = [nc.dram_tensor(name, v.shape, mybir.dt.from_np(v.dtype), kind="ExternalInput").ap()
            for name, v in arrays.items()]
    out = nc.dram_tensor("out", [TOK, H], F32, kind="ExternalOutput").ap()
    adaln_moe_kernel(nc, *args, out)
    r = run_bass_kernel_spmd(nc, [arrays], core_ids=[0])
    return r.results[0]["out"].reshape(B, S, H)
```

```python
from contextlib import ExitStack

import concourse.bass as bass
from concourse import mybir

F32 = mybir.dt.float32
BF16 = mybir.dt.bfloat16
F16 = mybir.dt.float16
I32 = mybir.dt.int32
U32 = mybir.dt.uint32
ALU = mybir.AluOpType
ACT = mybir.ActivationFunctionType
AX_X = mybir.AxisListType.X
RMAX = bass.bass_isa.ReduceOp.max

P = 128
B, S, H = 64, 64, 512
TOK = B * S
HK = H // P
D = 256
DM = D // P
E_SH, E_RT = 2, 16
K_TOP = 2
N_AD, RANK = 8, 16
AR = N_AD * RANK
assert AR == P

CHUNK = 256
NT = CHUNK // P
NB = CHUNK // S
NC = TOK // CHUNK
TT = TOK // P
EM = E_SH * DM
EARLY = 6
LATE = NC - EARLY
NJ = (TOK * K_TOP + E_RT * (P - 1)) // P
NJ_2 = NJ // 2
NJ_ALL = NJ + 1
assert NJ % 2 == 1
GRP = 8
NG = TT // GRP * K_TOP
WU, WD = HK * D, DM * H
UP_HI, UP_LO, DN_HI, DN_LO = 0, WU, 2 * WU, 2 * WU + WD
WE = 2 * (WU + WD)
SPLITS = 2 * (E_RT + 1)
A_HALF = NC // 2
SCALED = LIN_W, LIN_A, SH_UP, SH_DN, RT_UP, RT_DN, C_EARLY, C_ALL = range(8)
SH_FIRST, SH_REST, ROUTED = range(3)
EXP_ONE = 1 << 23
TOP = 14
BIAS = 127
HEAD = 2 * (TOP + 1) + H.bit_length() - 1 - (TOP + 1)
assert EARLY == NC - EARLY - 4 and EARLY <= A_HALF and NC % 4 == 0 and NC == E_RT and EM == HK and NG == 8


def adaln_moe_kernel(nc, xT, x_rows, idx, WT, AT, BmT, scal, sh_up, sh_dn, rt_w, w_r, out):
    ctx = ExitStack()
    with ctx:
        def sb(name, shape, dt=F32):
            return ctx.enter_context(nc.sbuf_tensor(name, shape, dt))

        def sem(name):
            return ctx.enter_context(nc.semaphore(name))

        def sems(name, n=2):
            return [sem(f"{name}{s}") for s in range(n)]

        xc_dram = nc.dram_tensor("xc_dram", [TOK, H], F32, kind="Internal").ap()
        xcT_dram = nc.dram_tensor("xcT_dram", [NC, P, HK * CHUNK], F32, kind="Internal").ap()
        s_dram = nc.dram_tensor("s_dram", [TOK, H], F32, kind="Internal").ap()
        r_dram = nc.dram_tensor("r_dram", [NJ * P, H], F32, kind="Internal").ap()

        shw = sb("shw", [P, E_SH, WE], F16)
        rtw = sb("rtw", [P, E_RT + 1, WE], F16)

        def arrived(e):
            return rtw[:, bass.ds(e, 1), :].rearrange("p a n -> p (a n)").bitcast(F32)

        w_place, a_place = 13, 14
        w_in = arrived(w_place).rearrange("p (k h) -> p k h", k=HK)
        at_in = arrived(a_place)[:, 0:HK * AR].rearrange("p (k r) -> p k r", k=HK)
        spare = rtw[:, E_RT, :].bitcast(F32)
        condT_in = spare[:, 0:HK * CHUNK]
        xres = spare[:, HK * CHUNK:].rearrange("p (t h) -> p t h", t=NT)
        act_in = [sb(f"act_in{s}", [P, HK, CHUNK]) for s in range(2)]
        rows = [sb(f"rows{s}", [P, NT, H]) for s in range(2)]
        hid = [sb(f"hid{s}", [P, HK, CHUNK]) for s in range(2)]
        xam = [sb(f"xam{s}", [P, CHUNK]) for s in range(2)]
        actT = [v[:].rearrange("p k t -> p (k t)").bitcast(F16).rearrange("p (a k t) -> p a k t", a=2, k=HK) for v in act_in]
        hidT = [v[:].rearrange("p k t -> p (k t)").bitcast(F16).rearrange("p (a k t) -> p a k t", a=2, k=EM) for v in hid]
        arena = sb("arena", [P, HK * CHUNK])
        tmp = sb("tmp", [P, EM * CHUNK])
        mid = [tmp[:, s * D:(s + 1) * D] for s in range(2)]
        xp = [v[:].bitcast(F16).rearrange("p (a k t) -> p a k t", a=2, k=HK) for v in (tmp, arena)]
        midT = [tmp[:, (2 + s) * D:(3 + s) * D].bitcast(F16).rearrange("p (a m t) -> p a m t", a=2, m=DM) for s in range(2)]

        region = sb("region", [P, HK * H + HK * AR + H + HK * E_RT])

        def carve(sizes):
            at, views = 0, []
            for shape, dt in sizes:
                n = 1
                for d in shape:
                    n *= d
                words = n * (4 if dt is F32 else 2) // 4
                v = region[:, at:at + words]
                at += words
                if dt is not F32:
                    v = v.bitcast(dt)
                if len(shape) == 2:
                    v = v.rearrange("p (a b) -> p a b", a=shape[0])
                if len(shape) == 3:
                    v = v.rearrange("p (a b c) -> p a b c", a=shape[0], b=shape[1])
                views.append(v)
            assert at <= HK * H + HK * AR + H + HK * E_RT
            return views

        wt, at_, bmt, wr = carve([((2, HK, H), F16), ((2, HK, AR), F16), ((H,), F32), ((HK, E_RT), F32)])
        acc0, acc1, pref = carve([((TT, E_RT), F32)] * 3)
        inv_bufs = carve([((GRP, P), F16), ((GRP, NJ_ALL), F16)] * 2)
        in_part, in_val = inv_bufs[0::2], inv_bufs[1::2]
        routed_bufs = carve([((H,), F32), ((2, HK, P), F16), ((H,), F32)] * 2)
        xg, xgT, rrow = routed_bufs[0::3], routed_bufs[1::3], routed_bufs[2::3]

        late = rtw[:].rearrange("p e n -> p (e n)").bitcast(F32)
        assert (NC + 4 * K_TOP) * NT * H + (2 * HK + EM) * CHUNK <= E_RT * WE // 2

        def sum_rows(c, n=1):
            return late[:, bass.ds(c * NT * H, n * NT * H)].rearrange("p (t h) -> p t h", h=H)

        def routed_row(slot, r, t):
            at = ((NC + slot * K_TOP + r) * NT + t) * H
            return late[:, at:at + H]


        ident = sb("ident", [P, P])
        lower = sb("lower", [P, P], BF16)
        ones = sb("ones", [P, P], BF16)
        iota_p = sb("iota_p", [P, P], F16)
        iota_j = sb("iota_j", [P, NJ_ALL], F16)
        iota_e = sb("iota_e", [P, E_RT])
        tok_no = sb("tok_no", [P, TT])
        part_i = sb("part_i", [P, 1], I32)
        part_f = sb("part_f", [P, 1])
        ad_i = sb("ad_i", [P, 1], I32)
        ad_f = sb("ad_f", [P, 1])
        sc_col = sb("sc_col", [P, 1])
        warm = sb("warm", [P, 1])
        idx_b = sb("idx_b", [P, B], I32)
        mask = sb("mask", [P, B])
        lg = sb("lg", [P, TT, E_RT])
        lg_c = [sb(f"lg_c{s}", [P, NT, E_RT]) for s in range(2)]
        best_c = [sb(f"best_c{s}", [P, NT, 8]) for s in range(2)]
        best_i_c = [sb(f"best_i_c{s}", [P, NT, 8], U32) for s in range(2)]
        best = sb("best", [P, TT, K_TOP])
        zsum = sb("zsum", [P, TT])
        gate = sb("gate", [P, K_TOP, TT])
        chosen = sb("chosen", [P, K_TOP, TT])
        words = TT * E_RT // 2
        oh = [arena[:, r * words:(r + 1) * words].bitcast(BF16).rearrange("p (t e) -> p t e", t=TT) for r in range(K_TOP + 1)]
        oh_sum = oh.pop()
        at = (K_TOP + 1) * words
        hi_i, lo_i, hi_f, lo_f = [arena[:, at + n * K_TOP * TT:at + (n + 1) * K_TOP * TT].bitcast(I32 if n < 2 else F32)
                                  .rearrange("p (r t) -> p r t", r=K_TOP) for n in range(4)]
        cnt_i = sb("cnt_i", [P, E_RT], I32)
        tiles_i = sb("tiles_i", [P, E_RT], I32)
        tiles_f = sb("tiles_f", [P, E_RT])
        end_t = [sb(f"end_t{s}", [P, E_RT]) for s in range(2)]
        start_s = sb("start_s", [P, E_RT])
        pos_f = sb("pos_f", [P, K_TOP, TT])
        pos = sb("pos", [P, K_TOP, TT], I32)
        past = sb("past", [P, E_RT])
        tile_col = sb("tile_col", [P, 1])
        tile_e = sb("tile_e", [1, NJ_ALL // 2, 4], I32)
        tok = sb("tok", [P, NJ_ALL], I32)
        lot_max = sb("lot_max", [P, 2, E_RT])
        c_chunk = sb("c_chunk", [P, NC])
        largest = sb("largest", [P, len(SCALED)])
        largest_all = sb("largest_all", [P, len(SCALED)])
        expo = sb("expo", [P, len(SCALED)], I32)
        neg_expo = sb("neg_expo", [P, len(SCALED)], I32)
        scale = sb("scale", [P, len(SCALED)], I32)
        unscale = sb("unscale", [P, len(SCALED)], I32)
        un_up, to_mid, un_dn = sb("un_up", [P, 3]), sb("to_mid", [P, 3]), sb("un_dn", [P, 3])

        x_max = [sb(f"x_max{s}", [P, 1]) for s in range(2)]
        x_max_all = [sb(f"x_max_all{s}", [P, 1]) for s in range(2)]
        x_expo = [sb(f"x_expo{s}", [P, 1], I32) for s in range(2)]
        x_unscale = [sb(f"x_unscale{s}", [P, 1], I32) for s in range(2)]
        x_scale = [sb(f"x_scale{s}", [P, 1], I32) for s in range(2)]
        un_cond = [sb(f"un_cond{s}", [P, 1]) for s in range(2)]
        w_to_a = sb("w_to_a", [P, 1])

        def col(v, n):
            return v[:, n:n + 1]

        slot_idx = [sb(f"slot_idx{s}", [P, 1], I32) for s in range(2)]
        row_idx = [sb(f"row_idx{s}", [P, K_TOP, NT], I32) for s in range(4)]

        bank = [ctx.enter_context(nc.psum_tensor(f"bank{i}", [P, 512], F32)) for i in range(8)]
        XA, COND, XPOSE, LOGIT = bank[0], bank[1:3], bank[3:5], bank[5]
        PRE, TOT, INV, TILE_E = bank[6], bank[7], bank[0], bank[5]
        UP, DOWN = bank[1:3], bank[3:5]
        R_XT, R_UP, R_MT, R_DN = [bank[0], bank[5]], bank[6:8], bank[2:0:-1], bank[3:5]

        w_adapters, w_mask, w_cond, w_shared = sem("w_adapters"), sem("w_mask"), sem("w_cond"), sem("w_shared")
        w_loaded = sems("w_loaded", 4)
        lot_max_ready, largest_ready, reduced, scale_ready, un_ready = (
            sem("lot_max_ready"), sem("largest_ready"), sem("reduced"), sem("scale_ready"), sem("un_ready"))
        w_half, w_split, c_chunk_ready = sem("w_half"), sem("w_split"), sem("c_chunk_ready")
        condT_loaded, condT_half, actT_ready = sems("condT_loaded"), sem("condT_half"), sem("actT_ready")
        hid_half, hid_ready = sem("hid_half"), sem("hid_ready")
        xgT_half, midT_half = sem("xgT_half"), sem("midT_half")
        iotas, masks, consts = sem("iotas"), sem("masks"), sem("consts")
        v_step = sem("v_step")
        lin_half, lin_split = sem("lin_half"), sem("lin_split")
        x_max_found, x_max_ready, x_reduced = sem("x_max_found"), sem("x_max_ready"), sem("x_reduced")
        x_expo_ready, x_scale_ready = sem("x_expo_ready"), sem("x_scale_ready")
        x_half, x_split = sem("x_half"), sem("x_split")
        act_loaded, act_used = sems("act_loaded"), sem("act_used")
        xa_ready, xam_ready = sem("xa_ready"), sem("xam_ready")
        cond_ready, rows_ready = sem("cond_ready"), sem("rows_ready")
        xpose_ready, condT_ready = sem("xpose_ready"), sem("condT_ready")
        rows_stored, condT_stored = sems("rows_stored"), sems("condT_stored")
        logit_ready, logit_copied, best_ready = sem("logit_ready"), sem("logit_copied"), sem("best_ready")
        place_found, top_ready = sem("place_found"), sem("top_ready")
        onehot_ready, prefix_ready = sem("onehot_ready"), sem("prefix_ready")
        shifted_ready, exp_ready = sem("shifted_ready"), sem("exp_ready")
        tile_col_ready, tile_row_ready = sem("tile_col_ready"), sem("tile_row_ready")
        place_ready, place_used, sorted_ready = sem("place_ready"), sem("place_used"), sem("sorted_ready")
        up_ready, gelu_ready = sem("up_ready"), sem("gelu_ready")
        down_ready, shared_ready = sem("down_ready"), sem("shared_ready")
        x_loaded, sum_ready = sem("x_loaded"), sem("sum_ready")
        idx_first, idx_ready = sem("idx_first"), sem("idx_ready")
        xg_loaded = sems("xg_loaded")
        xgT_psum, xgT_ready = sem("xgT_psum"), sem("xgT_ready")
        r_up_ready, r_gelu_ready = sem("r_up_ready"), sem("r_gelu_ready")
        midT_psum, midT_ready = sem("midT_psum"), sem("midT_ready")
        r_dn_ready, rrow_ready = sem("r_dn_ready"), sem("rrow_ready")
        rrow_stored = sems("rrow_stored")
        c_idx_first, c_idx_ready, e_idx_first, e_idx_ready = (
            sem("c_idx_first"), sem("c_idx_ready"), sem("e_idx_first"), sem("e_idx_ready"))
        y_loaded, e_loaded, c_r_loaded = sems("y_loaded"), sems("e_loaded"), sems("c_r_loaded", 4)
        half_weighed, weighed, e_half_weighed, e_weighed = (
            sem("half_weighed"), sem("weighed"), sem("e_half_weighed"), sem("e_weighed"))
        out_stored, e_stored = sem("out_stored"), sem("e_stored")

        block = ctx.enter_context(nc.Block())

        def flat(ap):
            return ap.rearrange("p k t -> p (k t)")

        def chunk_rows(dram, c):
            return dram[bass.ds(c * CHUNK, CHUNK), :].rearrange("(t p) h -> p t h", p=P)

        def chunk_T(dram, c):
            return dram[bass.ds(c, 1)].rearrange("a p n -> p (a n)")

        def tile_rows(dram, n):
            return dram[bass.ds(n * P, P), :]

        def early_condT(c):
            if c == 0:
                return tmp[:]
            return region[:, HK * H:HK * H + HK * CHUNK] if c % 2 == 0 and c < EARLY else condT_in

        def late_condT(s):
            at = (NC + 4 * K_TOP + s) * NT * H
            return late[:, at:at + HK * CHUNK]

        def late_tmp(s):
            at = (NC + 4 * K_TOP + 2) * NT * H
            return late[:, at:at + EM * CHUNK] if s else tmp[:]

        def by_block(v):
            return v.rearrange("p (k t) -> p k t", k=HK)

        def shared_w(u):
            at, n = ((UP_HI, UP_LO), (DN_HI, DN_LO))[u], (WU, WD)[u]
            return (lambda a: shw[:, :, at[a]:at[a] + n], (arrived(0), spare)[u].rearrange("p (e n) -> p e n", e=E_SH),
                    (SH_UP, SH_DN)[u])

        @block.sync
        def _(sp):
            sp.dma_start(at_in, AT).then_inc(w_adapters, 16)
            sp.dma_start(flat(act_in[0][:]), chunk_T(xT, 0)).then_inc(act_loaded[0], 16)
            sp.dma_start(sc_col[:], scal).then_inc(w_mask, 16)
            sp.dma_start(idx_b[:], idx.partition_broadcast(P)).then_inc(w_mask, 16)
            for dst, src in ((w_in, WT), (bmt, BmT), (wr, w_r)):
                sp.dma_start(dst, src).then_inc(w_cond, 16)
            sp.dma_start(flat(act_in[1][:]), chunk_T(xT, 1)).then_inc(act_loaded[1], 16)
            sp.dma_start(arrived(0), sh_up).then_inc(w_shared, 16)
            sp.dma_start(spare, sh_dn).then_inc(w_shared, 16)
            sp.wait_ge(act_used, 1)
            sp.dma_start(flat(act_in[0][:]), chunk_T(xT, 2)).then_inc(act_loaded[0], 16)
            for r in range(4):
                sp.dma_start(arrived(r + 1), rt_w[:, r, :]).then_inc(w_loaded[r], 16)

            def cond_chunk(i, s, more=True, first=False):
                c = 2 * i + s
                if more:
                    if first:
                        sp.wait_ge(act_used, 2)
                    else:
                        sp.wait_ge(x_split, c)
                    sp.dma_start(flat(act_in[1 - s][:]), chunk_T(xT, c + 3)).then_inc(act_loaded[1 - s], 16)
                sp.wait_ge(rows_ready, NT * c + NT)
                sp.dma_start(chunk_rows(xc_dram, c), rows[s][:]).then_inc(rows_stored[s], 16)
                sp.wait_ge(condT_ready, NT * c + NT)
                sp.dma_start(chunk_T(xcT_dram, c), flat(hid[s][:])).then_inc(condT_stored[s], 16)

            def weights_chunk(i, s):
                cond_chunk(i, s, first=(i == 0 and s == 0))
                for r in (2 * s, 2 * s + 1):
                    n = 4 * i + r
                    if n + 5 == w_place:
                        sp.wait_ge(act_used, 2)
                        sp.wait_ge(lin_split, 2)
                    if n + 5 == E_RT:
                        sp.wait_ge(w_split, 2)
                    sp.wait_ge(lot_max_ready, n + 1)
                    sp.dma_start(arrived(n + 5), rt_w[:, bass.ds(n + 4, 1), :].rearrange("p a n -> p (a n)")).then_inc(w_loaded[r], 16)

            for i in range(E_RT // 4 - 1):
                for s in range(2):
                    weights_chunk(i, s)
            with sp.Fori(E_RT // 4 - 1, A_HALF - 2) as i:
                for s in range(2):
                    cond_chunk(i, s)
            cond_chunk(A_HALF - 2, 0)
            cond_chunk(A_HALF - 2, 1, more=False)

            def load_condT(c, s, place):
                sp.dma_start(place, chunk_T(xcT_dram, c)).then_inc(condT_loaded[s], 16)

            def load_x(c):
                sp.dma_start(xres, chunk_rows(x_rows, c)).then_inc(x_loaded, 16)

            sp.wait_ge(condT_stored[0], 16)
            sp.wait_ge(act_used, NC - 1)
            load_condT(0, 0, early_condT(0))
            cond_chunk(A_HALF - 1, 0, more=False)
            sp.wait_ge(w_split, SPLITS)
            sp.wait_ge(condT_stored[1], 16)
            load_condT(1, 1, early_condT(1))
            load_x(0)
            cond_chunk(A_HALF - 1, 1, more=False)
            for s in range(2):
                sp.wait_ge(condT_stored[s], 16 * A_HALF)

            def next_condT(c):
                sp.wait_ge(actT_ready, c + 1 if c + 2 < EARLY else c + 2)
                load_condT(c + 2, c % 2, early_condT(c + 2))

            sp.wait_ge(cond_ready, TT)
            for c in range(2):
                next_condT(c)
            for c in range(EARLY):
                if c + 4 < EARLY:
                    next_condT(c + 2)
                if EARLY <= c + 3 < EARLY + 2:
                    next_condT(c + 1)
                sp.wait_ge(sum_ready, c + 1)
                sp.dma_start(chunk_rows(s_dram, c), rows[c % 2][:]).then_inc(rows_stored[c % 2], 16)
                if c + 1 < EARLY:
                    load_x(c + 1)

            def store_r(j, s):
                sp.wait_ge(rrow_ready, j + 1)
                sp.dma_start(tile_rows(r_dram, j), rrow[s]).then_inc(rrow_stored[s], 16)

            with sp.Fori(0, NJ_2) as i:
                for s in range(2):
                    store_r(2 * i + s, s)
            store_r(NJ - 1, 0)

            def load_y(c, s):
                sp.dma_start(sum_rows(c), chunk_rows(x_rows, c)).then_inc(y_loaded[s], 16)

            def late_loads(i, s):
                sp.wait_ge(actT_ready, 2 * i + s + 1)
                load_condT(2 * i + s + 2, s, late_condT(s))
                sp.wait_ge(y_loaded[s], 16 * (i - EARLY // 2 + 1))
                load_y(2 * i + s + 2, s)

            def store_sums(c):
                sp.wait_ge(weighed, c - EARLY + 1)
                sp.wait_ge(shared_ready, NT * c + NT)
                sp.dma_start(chunk_rows(out, c), sum_rows(c)).then_inc(out_stored, 16)

            def store_early(k, n):
                sp.wait_ge(e_weighed, k + n)
                sp.dma_start(out[k * CHUNK:(k + n) * CHUNK, :].rearrange("(t p) h -> p t h", p=P),
                             sum_rows(k, n)).then_inc(e_stored, 16)

            def load_early(k, s):
                sp.dma_start(sum_rows(k), chunk_rows(s_dram, k)).then_inc(e_loaded[s], 16)

            sp.wait_ge(r_dn_ready, NJ)
            for s in range(2):
                load_y(EARLY + s, s)
            for s in range(2):
                late_loads(EARLY // 2, s)
            for s in range(2):
                sp.wait_ge(rows_stored[s], 16 * (A_HALF + EARLY // 2))
            for s in range(2):
                load_early(s, s)
            store_sums(EARLY)
            with sp.Fori(EARLY // 2 + 1, A_HALF - 2) as i:
                for s in range(2):
                    late_loads(i, s)
                    sp.wait_ge(e_loaded[s], 16 * (i - EARLY // 2))
                    load_early(2 * i + s - EARLY, s)
                    store_sums(2 * i + s - 1)
            for s in range(2):
                late_loads(A_HALF - 2, s)
            store_early(0, 2)
            for s in range(2):
                store_sums(NC - 5 + s)
            store_sums(NC - 3)
            store_early(2, EARLY - 2)
            store_sums(NC - 2)
            sp.wait_ge(weighed, LATE)
            for n in range(TT - NT, TT):
                sp.wait_ge(shared_ready, n + 1)
                sp.dma_start(tile_rows(out, n), sum_rows(NC - 1)[:, n % NT, :]).then_inc(out_stored, 16)
            sp.wait_ge(out_stored, 16 * (LATE + NT - 1))
            sp.wait_ge(e_stored, 2 * 16)

        @block.gpsimd
        def _(pool):
            def iota(dst, n):
                nc.gpsimd.iota(dst, [[1, n]], base=0, channel_multiplier=0,
                               allow_small_or_imprecise_dtypes=True).then_inc(iotas, 1)

            nc.gpsimd.iota(part_i[:], [[0, 1]], base=0, channel_multiplier=1).then_inc(iotas, 1)
            iota(iota_p[:], P)
            iota(iota_j[:], NJ_ALL)
            iota(iota_e[:], E_RT)
            nc.gpsimd.iota(tok_no[:], [[P, TT]], base=-TOK // 2, channel_multiplier=1,
                           allow_small_or_imprecise_dtypes=True).then_inc(iotas, 1)
            nc.gpsimd.memset(ident[:], 0.0).then_inc(masks, 1)
            nc.gpsimd.memset(ones[:], 1.0).then_inc(masks, 1)
            nc.gpsimd.memset(lower[:], 1.0).then_inc(masks, 1)
            pool.wait_ge(masks, 3)
            nc.gpsimd.affine_select(out=ident[:], in_=ident[:], compare_op=ALU.not_equal, fill=1.0, base=0,
                                    pattern=[[-1, P]], channel_multiplier=1).then_inc(consts, 1)
            nc.gpsimd.affine_select(out=lower[:], in_=lower[:], compare_op=ALU.is_gt, fill=0.0, base=0,
                                    pattern=[[1, P]], channel_multiplier=-1).then_inc(consts, 1)

            def reduce_max(n, a, b):
                pool.wait_ge(largest_ready, n)
                nc.gpsimd.partition_all_reduce(largest_all[:, a:b], largest[:, a:b], P, RMAX).then_inc(reduced, 1)

            def x_reduce(c, s):
                pool.wait_ge(x_max_ready, c - 1)
                nc.gpsimd.partition_all_reduce(x_max_all[s][:], x_max[s][:], P, RMAX).then_inc(x_reduced, 1)

            def x_low(c, s):
                pool.wait_ge(x_half, c - 1)
                nc.gpsimd.tensor_tensor(un_cond[s][:], x_unscale[s][:].bitcast(F32), col(unscale, LIN_W).bitcast(F32), ALU.mult)
                nc.gpsimd.tensor_tensor(xp[s][:, 1], act_in[s][:], xp[s][:, 0], ALU.subtract).then_inc(x_split, 1)

            def low_shared(u):
                pool.wait_ge(w_half, u + 1)
                part, place, n = shared_w(u)
                nc.gpsimd.tensor_tensor(part(1), place, part(0), ALU.subtract).then_inc(w_split, 1)

            reduce_max(1, LIN_W, SH_UP)
            reduce_max(2, SH_UP, RT_UP)
            pool.wait_ge(scale_ready, 1)
            x_reduce(2, 0)
            for c in range(2, NC):
                x_low(c, c % 2)
                if c in (3, 4):
                    low_shared(c - 3)
                if c + 1 < NC:
                    x_reduce(c + 1, 1 - c % 2)
                if c == NC // 2:
                    reduce_max(3, RT_UP, C_ALL)

            def add_x(i, s):
                c = 2 * i + s
                pool.wait_ge(shared_ready, NT * c + NT)
                pool.wait_ge(x_loaded, 16 * (c + 1))
                nc.gpsimd.tensor_tensor(rows[s][:], rows[s][:], xres, ALU.add).then_inc(sum_ready, 1)

            def low_condT(c):
                pool.wait_ge(condT_half, c + 1)
                nc.gpsimd.tensor_tensor(actT[c % 2][:, 1], by_block(early_condT(c)), actT[c % 2][:, 0],
                                        ALU.subtract).then_inc(actT_ready, 1)

            def low_hid(c):
                pool.wait_ge(hid_half, c + 1)
                nc.gpsimd.tensor_tensor(hidT[c % 2][:, 1], by_block(tmp[:]), hidT[c % 2][:, 0],
                                        ALU.subtract).then_inc(hid_ready, 1)

            low_condT(0)
            low_condT(1)
            for c in range(EARLY - 2):
                low_hid(c)
                if c == 0:
                    reduce_max(4, C_ALL, C_ALL + 1)
                low_condT(c + 2)
                if c:
                    add_x((c - 1) // 2, (c - 1) % 2)
            low_hid(EARLY - 2)

            pool.wait_ge(sorted_ready, 1)
            for s in range(2):
                pool.wait_ge(rows_stored[s], 16 * A_HALF)

            def gather(i, s, first):
                j = 2 * i + s
                copied = idx_first if first else idx_ready
                if not first:
                    pool.wait_ge(xgT_psum, j - 1)
                nc.gpsimd.tensor_copy(slot_idx[s][:], tok[:, bass.ds(j, 1)]).then_inc(copied, 1)
                pool.wait_ge(sorted_ready, 1)
                pool.wait_ge(copied, j + 1 if first else j - 1)
                nc.gpsimd.indirect_dma_start(
                    out=xg[s], out_offset=None, in_=xc_dram,
                    in_offset=bass.IndirectOffsetOnAxis(ap=slot_idx[s][:].bitcast(U32), axis=0),
                ).then_inc(xg_loaded[s], 16)

            for s in range(2):
                gather(0, s, True)
            add_x((EARLY - 3) // 2, (EARLY - 3) % 2)
            low_hid(EARLY - 1)
            low_condT(EARLY)
            for s in range(2):
                gather(1, s, False)
            add_x((EARLY - 2) // 2, (EARLY - 2) % 2)
            for s in range(2):
                gather(2, s, False)
            add_x((EARLY - 1) // 2, (EARLY - 1) % 2)
            with pool.Fori(3, NJ_2) as i:
                for s in range(2):
                    gather(i, s, False)
            gather(NJ_2, 0, False)

            def gather_back(c, slot, n, first_copied, copied, used=None):
                if used is None:
                    copied, before = first_copied, n + 1
                else:
                    before = n - 1
                    pool.wait_ge(used, before)
                nc.gpsimd.tensor_copy(row_idx[slot][:], pos[:, :, bass.ds(c * NT, NT)]).then_inc(copied, 1)
                pool.wait_ge(sorted_ready, 1)
                pool.wait_ge(copied, before)
                for r in range(K_TOP):
                    for t in range(NT):
                        nc.gpsimd.indirect_dma_start(
                            out=routed_row(slot, r, t), out_offset=None, in_=r_dram,
                            in_offset=bass.IndirectOffsetOnAxis(ap=row_idx[slot][:, r, t:t + 1].bitcast(U32), axis=0),
                        ).then_inc(c_r_loaded[slot], 16)

            def gather_late(c, s, used=None):
                gather_back(c, s, c - EARLY, c_idx_first, c_idx_ready, used)

            def gather_early(k, s, used=None):
                gather_back(k, 2 + s, k, e_idx_first, e_idx_ready, used)

            pool.wait_ge(r_dn_ready, NJ)
            for s in range(2):
                pool.wait_ge(rrow_stored[s], 16 * (NJ_2 + 1 - s))
            for s in range(2):
                gather_late(EARLY + s, s)
            for s in range(2):
                gather_early(s, s)
            gather_late(EARLY + 2, 0, weighed)
            with pool.Fori(EARLY // 2 + 1, A_HALF - 2) as i:
                for s in range(2):
                    gather_late(2 * i + s + 1, 1 - s, weighed)
                    gather_early(2 * i + s - EARLY, s, e_weighed)
            gather_late(NC - 3, 1, weighed)
            for s in range(2):
                gather_back(NC - 2 + s, 2 + s, EARLY + s, e_idx_first, e_idx_ready, e_weighed)

        @block.scalar
        def _(act):
            def high(dst, src, n):
                nc.scalar.activation(dst, src, ACT.Copy, scale=col(scale, n).bitcast(F32)).then_inc(w_half, 1)

            def high_shared(u):
                part, place, n = shared_w(u)
                nc.scalar.activation(part(0), place, ACT.Copy, scale=col(scale, n).bitcast(F32))
                nc.scalar.activation(place, place, ACT.Copy, scale=col(scale, n).bitcast(F32)).then_inc(w_half, 1)

            def high_routed(e):
                act.wait_ge(w_split, 2 * e + 1)
                high(rtw[:, bass.ds(e, 1), UP_HI:UP_HI + WU].rearrange("p a n -> p (a n)"), arrived(e + 1)[:, 0:WU], RT_UP)
                act.wait_ge(w_split, 2 * e + 2)
                high(rtw[:, bass.ds(e, 1), DN_HI:DN_HI + WD].rearrange("p a n -> p (a n)"), arrived(e + 1)[:, WU:], RT_DN)

            def high_condT(c, s, n=C_ALL, early=False, place=None):
                act.wait_ge(condT_loaded[s], 8 * (c - s) + 16)
                if early and c < 2:
                    act.wait_ge(act_used, NC - 1 + c)
                else:
                    act.wait_ge(up_ready, EM * c - EM)
                src, by = place or (early_condT(c) if early else late_condT(s)), col(scale, n).bitcast(F32)
                last = nc.scalar.activation(actT[s][:, 0], by_block(src), ACT.Copy, scale=by)
                if early:
                    last = nc.scalar.activation(src, src, ACT.Copy, scale=by)
                last.then_inc(condT_half, 1)

            def high_linear(dst, src, n):
                nc.scalar.activation(dst, src, ACT.Copy, scale=col(scale, n).bitcast(F32)).then_inc(lin_half, 1)

            def high_x(c, s):
                act.wait_ge(x_scale_ready, c - 1)
                act.wait_ge(act_used, c - 1)
                by = x_scale[s][:].bitcast(F32)
                nc.scalar.activation(xp[s][:, 0], act_in[s][:], ACT.Copy, scale=by)
                nc.scalar.activation(act_in[s][:], act_in[s][:], ACT.Copy, scale=by).then_inc(x_half, 1)

            def cond_rows(i, s, first=False):
                c = 2 * i + s
                if not first:
                    act.wait_ge(rows_stored[s], 16 * i)
                    act.wait_ge(c_chunk_ready, c - 1)
                for t in range(NT):
                    act.wait_ge(cond_ready, NT * c + t + 1)
                    if first:
                        ins = nc.scalar.copy(rows[s][:, t, :], COND[t][:])
                    else:
                        ins = nc.scalar.activation(rows[s][:, t, :], COND[t][:], ACT.Copy, scale=un_cond[s][:])
                    ins.then_inc(rows_ready, 1)

            def cond_T(c, i, s, first=False):
                if not first:
                    act.wait_ge(condT_stored[s], 16 * i)
                act.wait_ge(xpose_ready, NT * c + NT)
                nc.scalar.copy(hid[s][:, :, CHUNK - P:], XPOSE[NT - 1][:].rearrange("p (k t) -> p k t", k=HK)).then_inc(condT_ready, 1)

            def cond_step(i, s, first=False):
                c = 2 * i + s
                cond_T(c - 1, i - 1 + s, 1 - s, first)
                cond_rows(i, s, first and s)

            act.wait_ge(scale_ready, 1)
            high_linear(wt[:, 0], w_in, LIN_W)
            high_linear(at_[:, 0], at_in, LIN_A)
            cond_rows(0, 0, first=True)
            high_x(2, 0)
            cond_step(0, 1, first=True)
            high_x(3, 1)
            cond_T(1, 0, 1, first=True)
            act.wait_ge(scale_ready, 2)
            high_shared(0)
            cond_rows(1, 0)
            high_x(4, 0)
            cond_T(2, 1, 0)
            high_shared(1)
            cond_rows(1, 1)
            with act.Fori(2, A_HALF // 2) as i:
                for s in range(2):
                    high_x(2 * i + s + 1, 1 - s)
                    cond_step(i, s)
            high_x(NC // 2 + 1, 1)
            act.wait_ge(scale_ready, 3)
            high_routed(0)
            cond_T(NC // 2 - 1, A_HALF // 2 - 1, 1)
            high_routed(1)
            cond_rows(A_HALF // 2, 0)

            def routed_step(i, s):
                high_routed(4 * i - NC + 2 * s)
                high_x(2 * i + s + 1, 1 - s)
                high_routed(4 * i - NC + 2 * s + 1)
                cond_step(i, s)

            routed_step(A_HALF // 2, 1)
            with act.Fori(A_HALF // 2 + 1, A_HALF - 1) as i:
                for s in range(2):
                    routed_step(i, s)
            for s in range(2):
                high_routed(E_RT - 4 + 2 * s)
                if s == 0:
                    high_x(NC - 1, 1)
                high_routed(E_RT - 3 + 2 * s)
                if s:
                    high_condT(0, 0, C_EARLY, early=True)
                cond_step(A_HALF - 1, s)

            cond_T(NC - 1, A_HALF - 1, 1)

            def gelus(c, s, n=SH_REST, early=False, blocks=range(EM)):
                if early and c == 0:
                    act.wait_ge(actT_ready, 1)
                else:
                    act.wait_ge(hid_ready, c if early else c - 1)
                place = tmp[:] if early else late_tmp(s)
                for em in blocks:
                    act.wait_ge(up_ready, EM * c + em + 1)
                    nc.scalar.activation(place[:, em * CHUNK:(em + 1) * CHUNK], UP[em % 2][:, 0:CHUNK], ACT.Gelu,
                                         scale=col(un_up, n)).then_inc(gelu_ready, 1)

            def high_hid(c, s, n=SH_REST, early=False):
                place = tmp[:] if early else late_tmp(s)
                if early and c < 2:
                    act.wait_ge(condT_stored[s], 16 * A_HALF)
                else:
                    act.wait_ge(down_ready, NT * c - NT)
                act.wait_ge(gelu_ready, EM * c + EM)
                last = nc.scalar.activation(hidT[s][:, 0], by_block(place), ACT.Copy, scale=col(to_mid, n))
                if early:
                    last = nc.scalar.activation(place, place, ACT.Copy, scale=col(to_mid, n))
                last.then_inc(hid_half, 1)

            def shared_rows(c):
                i, s, n = c // 2, c % 2, SH_FIRST
                act.wait_ge(rows_stored[s], 16 * (A_HALF + i))
                for t in range(NT):
                    act.wait_ge(down_ready, NT * c + t + 1)
                    nc.scalar.activation(rows[s][:, t, :], DOWN[t][:], ACT.Copy, scale=col(un_dn, n)).then_inc(shared_ready, 1)

            act.wait_ge(un_ready, 1)
            nc.scalar.activation(warm[:], sc_col[:], ACT.Gelu)
            gelus(0, 0, SH_FIRST, early=True, blocks=range(2))
            high_condT(1, 1, C_EARLY, early=True)
            for c in range(EARLY):
                gelus(c, c % 2, SH_FIRST, early=True, blocks=range(2 if c < 2 else 0, EM))
                high_hid(c, c % 2, SH_FIRST, early=True)
                if c == 0:
                    gelus(1, 1, SH_FIRST, early=True, blocks=range(2))
                if c + 2 == EARLY:
                    act.wait_ge(scale_ready, 4)
                if c < EARLY - 1:
                    high_condT(c + 2, c % 2, C_EARLY if c + 2 < EARLY else C_ALL, early=True)
                if c == 1:
                    act.wait_ge(c_chunk_ready, NC)
                if c:
                    shared_rows(c - 1)
            act.wait_ge(shifted_ready, 1)
            nc.scalar.activation(lg[:], lg[:], ACT.Exp)
            nc.scalar.activation(best[:, :, 1:2], best[:, :, 1:2], ACT.Exp).then_inc(exp_ready, 1)
            nc.scalar.activation(warm[:], sc_col[:], ACT.Gelu)
            act.wait_ge(un_ready, 3)

            def r_gelu(j, s):
                act.wait_ge(r_up_ready, j + 1)
                nc.scalar.activation(mid[s], R_UP[s][:, 0:D], ACT.Gelu, scale=col(un_up, ROUTED)).then_inc(r_gelu_ready, 1)

            def r_high(j, s):
                act.wait_ge(xgT_psum, j + 1)
                nc.scalar.activation(xgT[s][:, 0], R_XT[s][:].rearrange("p (k t) -> p k t", k=HK), ACT.Copy,
                                     scale=col(scale, C_ALL).bitcast(F32)).then_inc(xgT_half, 1)

            def r_rows(j, i, s, first=False):
                if not first:
                    act.wait_ge(rrow_stored[s], 16 * i)
                act.wait_ge(r_dn_ready, j + 1)
                nc.scalar.activation(rrow[s], R_DN[s][:], ACT.Copy, scale=col(un_dn, ROUTED)).then_inc(rrow_ready, 1)

            def r_step(j, i, s, first=False):
                r_gelu(j, s)
                r_high(j + 2, s)
                if not (first and j == 0):
                    r_rows(j - 1, i - 1 + s, 1 - s, first and j < 3)

            for s in range(2):
                r_high(s, s)
            shared_rows(EARLY - 1)
            for j in range(4):
                r_step(j, j // 2, j % 2, first=True)
            with act.Fori(2, NJ_2 - 1) as i:
                for s in range(2):
                    r_step(2 * i + s, i, s)
            r_step(NJ - 3, NJ_2 - 1, 0)
            high_condT(EARLY + 1, 1, place=early_condT(EARLY + 1))
            for j in range(NJ - 2, NJ):
                r_gelu(j, j % 2)
                r_rows(j - 1, (j - 1) // 2, (j - 1) % 2)
            r_rows(NJ - 1, NJ_2, 0)

            def late_step(c, s):
                gelus(c + 1, 1 - s)
                high_condT(c + 2, s)
                high_hid(c + 1, 1 - s)

            gelus(EARLY, 0)
            high_hid(EARLY, 0)
            for s in range(2):
                late_step(EARLY + s, s)
            with act.Fori(EARLY // 2 + 1, A_HALF - 1) as i:
                for s in range(2):
                    late_step(2 * i + s, s)
            gelus(NC - 1, 1)
            high_hid(NC - 1, 1)

        @block.vector
        def _(dve):
            steps = [0]

            def link(ins):
                steps[0] += 1
                ins.then_inc(v_step, 1)
                dve.wait_ge(v_step, steps[0])

            dve.wait_ge(w_mask, 2 * 16)
            dve.wait_ge(iotas, 5)
            link(nc.vector.tensor_scalar(ad_i[:], part_i[:], RANK.bit_length() - 1, None, ALU.logical_shift_right))
            link(nc.vector.tensor_copy(ad_f[:], ad_i[:]))
            link(nc.vector.tensor_copy(part_f[:], part_i[:]))
            link(nc.vector.tensor_scalar(mask[:], idx_b[:], ad_f[:], sc_col[:], ALU.is_equal, ALU.mult))

            def mask_xa(c, s):
                dve.wait_ge(xa_ready, c + 1)
                nc.vector.tensor_tensor(
                    xam[s][:].rearrange("p (b t) -> p b t", b=NB), XA[:, 0:CHUNK].rearrange("p (b t) -> p b t", b=NB),
                    mask[:, bass.ds(c * NB, NB)].unsqueeze(2).to_broadcast([P, NB, S]), ALU.mult,
                ).then_inc(xam_ready, 1)

            def cond_T(c, i, s, first=False):
                if not first:
                    dve.wait_ge(condT_stored[s], 16 * i)
                for t in range(NT - 1):
                    dve.wait_ge(xpose_ready, NT * c + t + 1)
                    nc.vector.tensor_copy(hid[s][:, :, t * P:(t + 1) * P],
                                          XPOSE[t][:].rearrange("p (k t) -> p k t", k=HK)).then_inc(condT_ready, 1)

            def top(c, s):
                dve.wait_ge(logit_ready, c + 1)
                nc.vector.tensor_copy(lg_c[s][:], LOGIT[:, 0:NT * E_RT].rearrange("p (t e) -> p t e", t=NT)).then_inc(logit_copied, 1)
                dve.wait_ge(logit_copied, c + 1)
                nc.vector.tensor_copy(lg[:, bass.ds(c * NT, NT), :], lg_c[s][:])
                for t in range(NT):
                    nc.vector.max(best_c[s][:, t, :], lg_c[s][:, t, :]).then_inc(best_ready, 1)
                dve.wait_ge(best_ready, c * NT + NT)
                nc.vector.tensor_copy(best[:, bass.ds(c * NT, NT), :], best_c[s][:, :, 0:K_TOP])
                for t in range(NT):
                    nc.vector.max_index(best_i_c[s][:, t, :], best_c[s][:, t, :], lg_c[s][:, t, :]).then_inc(place_found, 1)
                dve.wait_ge(place_found, c * NT + NT)
                nc.vector.tensor_copy(chosen[:, :, bass.ds(c * NT, NT)],
                                      best_i_c[s][:, :, 0:K_TOP].rearrange("p t r -> p r t")).then_inc(top_ready, 1)

            def row_max(c, s):
                dve.wait_ge(rows_ready, NT * c + NT)
                nc.vector.tensor_reduce(c_chunk[:, bass.ds(c, 1)], rows[s][:].rearrange("p t h -> p (t h)"), AX_X, ALU.max,
                                        apply_absolute_value=True).then_inc(c_chunk_ready, 1)

            def lot_maxima(at):
                i, r = at
                e = 4 * i + r
                dve.wait_ge(w_loaded[r], 16 * (i + 1))
                nc.vector.tensor_reduce(lot_max[:, :, bass.ds(e, 1)].rearrange("p u a -> p (u a)"),
                                        arrived(e + 1).rearrange("p (u n) -> p u n", u=2), AX_X, ALU.max,
                                        apply_absolute_value=True).then_inc(lot_max_ready, 1)

            def scales(n, a, b):
                dve.wait_ge(reduced, n)
                link(nc.vector.tensor_scalar(expo[:, a:b], largest_all[:, a:b].bitcast(I32), 255 * EXP_ONE, None, ALU.bitwise_and))
                link(nc.vector.tensor_scalar(neg_expo[:, a:b], expo[:, a:b], float(30 * EXP_ONE), -1.0, ALU.max, ALU.mult))
                link(nc.vector.tensor_scalar(unscale[:, a:b], neg_expo[:, a:b], -1.0, float(-TOP * EXP_ONE), ALU.mult, ALU.add))
                nc.vector.tensor_scalar(scale[:, a:b], neg_expo[:, a:b], float((TOP + 2 * BIAS) * EXP_ONE), None,
                                        ALU.add).then_inc(scale_ready, 1)

            def result_scales(n, c, up, dn):
                link(nc.vector.tensor_tensor(col(un_up, n), col(unscale, c).bitcast(F32), col(unscale, up).bitcast(F32), ALU.mult))
                nc.vector.tensor_scalar(col(to_mid, n).bitcast(I32), col(un_up, n).bitcast(I32), -1.0,
                                        float((2 * BIAS - HEAD) * EXP_ONE), ALU.mult, ALU.add)
                nc.vector.scalar_tensor_tensor(col(un_dn, n), col(un_up, n), float(1 << HEAD), col(unscale, dn).bitcast(F32),
                                               ALU.mult, ALU.mult).then_inc(un_ready, 1)

            def low(dst, src, n, hi, half):
                dve.wait_ge(w_half, half)
                nc.vector.scalar_tensor_tensor(dst, src, col(scale, n).bitcast(F32), hi, ALU.mult, ALU.subtract).then_inc(w_split, 1)

            def low_routed(e):
                def part(at):
                    return rtw[:, bass.ds(e, 1), at:at + WU].rearrange("p a n -> p (a n)")

                low(part(UP_LO), arrived(e + 1)[:, 0:WU], RT_UP, part(UP_HI), 2 * e + 3)
                low(part(DN_LO), arrived(e + 1)[:, WU:], RT_DN, part(DN_HI), 2 * e + 4)

            def x_largest(i, s):
                dve.wait_ge(act_loaded[s], 16 * (i + 1))
                nc.vector.tensor_reduce(x_max[s][:], flat(act_in[s][:]), AX_X, ALU.max, apply_absolute_value=True).then_inc(x_max_found, 1)
                dve.wait_ge(x_max_found, 2 * i + s - 1)
                nc.vector.tensor_scalar(x_max[s][:].bitcast(I32), x_max[s][:].bitcast(I32), 255 * EXP_ONE, None,
                                        ALU.bitwise_and).then_inc(x_max_ready, 1)

            def x_scales(c, s):
                dve.wait_ge(x_reduced, c - 1)
                nc.vector.tensor_scalar(x_expo[s][:], x_max_all[s][:].bitcast(I32), float(30 * EXP_ONE), None,
                                        ALU.max).then_inc(x_expo_ready, 1)
                dve.wait_ge(x_expo_ready, c - 1)
                nc.vector.tensor_scalar(x_unscale[s][:], x_expo[s][:], float(-TOP * EXP_ONE), None, ALU.add)
                nc.vector.tensor_scalar(x_scale[s][:], x_expo[s][:], -1.0, float((TOP + 2 * BIAS) * EXP_ONE),
                                        ALU.mult, ALU.add).then_inc(x_scale_ready, 1)

            def search_step(i, s, lots, first=False, masked=False):
                if not masked:
                    mask_xa(2 * i + s, s)
                row_max(2 * i + s - 1, 1 - s)
                c = 2 * i + s
                if not masked:
                    lot_maxima(lots[0])
                cond_T(c - 1, i - 1 + s, 1 - s, first)
                for at in lots[0 if masked else 1:]:
                    lot_maxima(at)
                if masked:
                    top(c - 1, 1 - s)
                x_largest(i + 1, s)
                if not masked:
                    top(c - 1, 1 - s)
                x_scales(c + 2, s)

            def low_linear(dst, src, n, hi, half):
                dve.wait_ge(lin_half, half)
                nc.vector.scalar_tensor_tensor(dst, src, col(scale, n).bitcast(F32), hi, ALU.mult, ALU.subtract).then_inc(lin_split, 1)

            mask_xa(0, 0)
            dve.wait_ge(w_cond, 3 * 16)
            dve.wait_ge(w_adapters, 16)
            nc.vector.tensor_reduce(col(largest, LIN_W), arrived(w_place), AX_X, ALU.max, apply_absolute_value=True)
            nc.vector.tensor_reduce(col(largest, LIN_A), arrived(a_place)[:, 0:HK * AR], AX_X, ALU.max,
                                    apply_absolute_value=True).then_inc(largest_ready, 1)
            scales(1, LIN_W, SH_UP)
            dve.wait_ge(w_shared, 2 * 16)
            nc.vector.tensor_reduce(col(largest, SH_UP), arrived(0), AX_X, ALU.max, apply_absolute_value=True)
            nc.vector.tensor_reduce(col(largest, SH_DN), spare, AX_X, ALU.max,
                                    apply_absolute_value=True).then_inc(largest_ready, 1)
            mask_xa(1, 1)
            low_linear(wt[:, 1], w_in, LIN_W, wt[:, 0], 1)
            low_linear(at_[:, 1], at_in, LIN_A, at_[:, 0], 2)
            dve.wait_ge(scale_ready, 1)
            link(nc.vector.tensor_tensor(w_to_a[:], col(scale, LIN_W).bitcast(F32), col(unscale, LIN_A).bitcast(F32), ALU.mult))
            link(nc.vector.tensor_scalar(mask[:], mask[:], w_to_a[:], None, ALU.mult))
            x_largest(1, 0)
            x_scales(2, 0)
            search_step(0, 1, [(0, 0), (0, 1)], first=True, masked=True)
            scales(2, SH_UP, RT_UP)
            search_step(1, 0, [(0, 2), (0, 3), (1, 0)], first=True)
            search_step(1, 1, [(1, 1), (1, 2), (1, 3)])
            with dve.Fori(2, A_HALF // 2) as i:
                for s in range(2):
                    search_step(i, s, [(i, 2 * s), (i, 2 * s + 1)])
            dve.wait_ge(c_chunk_ready, EARLY)
            dve.wait_ge(lot_max_ready, E_RT)
            nc.vector.tensor_reduce(largest[:, RT_UP:RT_DN + 1], lot_max[:], AX_X, ALU.max)
            nc.vector.tensor_reduce(col(largest, C_EARLY), c_chunk[:, 0:EARLY], AX_X, ALU.max).then_inc(largest_ready, 1)
            scales(3, RT_UP, C_ALL)
            result_scales(SH_FIRST, C_EARLY, SH_UP, SH_DN)
            def low_step(i, s, first=False, more=True):
                c = 2 * i + s
                mask_xa(c, s)
                row_max(c - 1, 1 - s)
                if first:
                    cond_T(c - 1, i - 1 + s, 1 - s)
                low_routed(2 * c - NC)
                if not first:
                    cond_T(c - 1, i - 1 + s, 1 - s)
                low_routed(2 * c - NC + 1)
                if more:
                    x_largest(i + 1, s)
                top(c - 1, 1 - s)
                if more:
                    x_scales(c + 2, s)

            for s in range(2):
                low_step(A_HALF // 2, s, first=(s == 0))
            with dve.Fori(A_HALF // 2 + 1, A_HALF - 1) as i:
                for s in range(2):
                    low_step(i, s)
            for s in range(2):
                low_step(A_HALF - 1, s, more=False)
            cond_T(NC - 1, A_HALF - 1, 1)
            top(NC - 1, 1)
            dve.wait_ge(top_ready, NC)

            for r in range(K_TOP):
                link(nc.vector.tensor_tensor(oh[r][:], iota_e[:].unsqueeze(1).to_broadcast([P, TT, E_RT]),
                                             chosen[:, r, :].unsqueeze(2).to_broadcast([P, TT, E_RT]), ALU.is_equal))
            nc.vector.tensor_tensor(oh_sum[:], oh[0][:], oh[1][:], ALU.add).then_inc(onehot_ready, 1)

            row_max(NC - 1, 1)
            dve.wait_ge(c_chunk_ready, NC)
            nc.vector.tensor_reduce(col(largest, C_ALL), c_chunk[:], AX_X, ALU.max).then_inc(largest_ready, 1)

            link(nc.vector.tensor_tensor(lg[:], lg[:], best[:, :, 0:1].to_broadcast([P, TT, E_RT]), ALU.subtract))
            nc.vector.tensor_tensor(best[:, :, 1:2], best[:, :, 1:2], best[:, :, 0:1], ALU.subtract).then_inc(shifted_ready, 1)

            dve.wait_ge(prefix_ready, 1)
            link(nc.vector.tensor_copy(acc0, TOT[:].rearrange("p (t e) -> p t e", t=TT)))
            src, dst, d = acc0, acc1, 1
            while d < TT:
                nc.vector.tensor_copy(dst[:, 0:d, :], src[:, 0:d, :])
                link(nc.vector.tensor_tensor(dst[:, d:, :], src[:, d:, :], src[:, :TT - d, :], ALU.add))
                src, dst, d = dst, src, 2 * d
            link(nc.vector.tensor_scalar(cnt_i[:], src[:, TT - 1, :], float(P - 1), None, ALU.add))
            link(nc.vector.tensor_scalar(tiles_i[:], cnt_i[:], P.bit_length() - 1, None, ALU.logical_shift_right))
            link(nc.vector.tensor_copy(tiles_f[:], tiles_i[:]))
            link(nc.vector.tensor_copy(end_t[0][:], tiles_f[:]))
            a, b, d = end_t[0], end_t[1], 1
            while d < E_RT:
                nc.vector.tensor_copy(b[:, 0:d], a[:, 0:d])
                link(nc.vector.tensor_tensor(b[:, d:], a[:, d:], a[:, :E_RT - d], ALU.add))
                a, b, d = b, a, 2 * d
            link(nc.vector.tensor_tensor(start_s[:], a[:], tiles_f[:], ALU.subtract))
            link(nc.vector.tensor_scalar(start_s[:], start_s[:], float(P), None, ALU.mult))
            link(nc.vector.tensor_scalar(past[:], a[:], part_f[:], None, ALU.is_le))
            link(nc.vector.tensor_reduce(tile_col[:], past[:], AX_X, ALU.add))
            nc.vector.tensor_scalar(tile_col[:], tile_col[:], float(E_RT - 1), None, ALU.min).then_inc(tile_col_ready, 1)
            link(nc.vector.tensor_tensor(dst, src, TOT[:].rearrange("p (t e) -> p t e", t=TT), ALU.subtract))
            link(nc.vector.tensor_tensor(pref, dst, PRE[:].rearrange("p (t e) -> p t e", t=TT), ALU.add))
            link(nc.vector.tensor_tensor(pref, pref, start_s[:].unsqueeze(1).to_broadcast([P, TT, E_RT]), ALU.add))
            for r in range(K_TOP):
                link(nc.vector.tensor_tensor(acc0, oh[r][:], pref, ALU.mult))
                link(nc.vector.tensor_reduce(pos_f[:, r, :], acc0, AX_X, ALU.add))
            link(nc.vector.tensor_copy(pos[:], pos_f[:]))
            link(nc.vector.tensor_scalar(hi_i[:], pos[:], P.bit_length() - 1, None, ALU.logical_shift_right))
            link(nc.vector.tensor_scalar(lo_i[:], pos[:], P - 1, None, ALU.bitwise_and))
            link(nc.vector.tensor_copy(hi_f[:], hi_i[:]))
            link(nc.vector.tensor_copy(lo_f[:], lo_i[:]))

            scales(4, C_ALL, C_ALL + 1)
            result_scales(SH_REST, C_ALL, SH_UP, SH_DN)
            result_scales(ROUTED, C_ALL, RT_UP, RT_DN)

            def places(i, first=False):
                for s in range(2):
                    if not first:
                        dve.wait_ge(place_used, 2 * i + s - 1)
                    for n in range(GRP):
                        at = bass.ds(i * GRP + n, 1)
                        nc.vector.tensor_scalar(in_part[s][:, n, :], iota_p[:], lo_f[:, s, at], None, ALU.is_equal)
                        last = nc.vector.tensor_scalar(in_val[s][:, n, :], iota_j[:], hi_f[:, s, at], tok_no[:, at],
                                                       ALU.is_equal, ALU.mult)
                    last.then_inc(place_ready, 1)

            places(0, first=True)
            with dve.Fori(1, NG // 2) as i:
                places(i)
            dve.wait_ge(tile_row_ready, 1)
            for n in (0, 2):
                nc.vector.tensor_copy(tile_e[:, :, n:n + 2], TILE_E[0:1, n:n + NJ_ALL].rearrange("p (i m) -> p i m", m=2))
            dve.wait_ge(place_used, NG)
            nc.vector.tensor_scalar(tok[:], INV[:, 0:NJ_ALL], float(TOK // 2), None, ALU.add).then_inc(sorted_ready, 1)

            def low_condT(c, s, place=None):
                dve.wait_ge(condT_half, c + 1)
                nc.vector.scalar_tensor_tensor(actT[s][:, 1], by_block(place or late_condT(s)), col(scale, C_ALL).bitcast(F32),
                                               actT[s][:, 0], ALU.mult, ALU.subtract).then_inc(actT_ready, 1)

            def low_xgT(j, s):
                dve.wait_ge(xgT_half, j + 1)
                nc.vector.scalar_tensor_tensor(xgT[s][:, 1], R_XT[s][:].rearrange("p (k t) -> p k t", k=HK),
                                               col(scale, C_ALL).bitcast(F32), xgT[s][:, 0], ALU.mult, ALU.subtract).then_inc(xgT_ready, 1)

            def split_midT(j, s):
                dve.wait_ge(midT_psum, j + 1)
                src = R_MT[s][:, 0:D].rearrange("p (m t) -> p m t", m=DM)
                nc.vector.tensor_scalar(midT[s][:, 0], src, col(to_mid, ROUTED), None, ALU.mult).then_inc(midT_half, 1)
                dve.wait_ge(midT_half, j + 1)
                nc.vector.scalar_tensor_tensor(midT[s][:, 1], src, col(to_mid, ROUTED), midT[s][:, 0],
                                               ALU.mult, ALU.subtract).then_inc(midT_ready, 1)

            for s in range(2):
                low_xgT(s, s)
            with dve.Fori(0, NJ_2 - 1) as i:
                for s in range(2):
                    low_xgT(2 * i + s + 2, s)
                    split_midT(2 * i + s, s)
            low_xgT(NJ - 1, 0)
            split_midT(NJ - 3, 0)
            low_condT(EARLY + 1, 1, early_condT(EARLY + 1))
            for j in range(NJ - 2, NJ):
                split_midT(j, j % 2)

            dve.wait_ge(exp_ready, 1)
            link(nc.vector.tensor_reduce(zsum[:], lg[:], AX_X, ALU.add))
            link(nc.vector.reciprocal(gate[:, 0, :], zsum[:]))
            link(nc.vector.tensor_tensor(gate[:, 1, :], gate[:, 0, :], best[:, :, 1], ALU.mult))

            def low_hid(c, s):
                dve.wait_ge(hid_half, c + 1)
                nc.vector.scalar_tensor_tensor(hidT[s][:, 1], by_block(late_tmp(s)), col(to_mid, SH_REST),
                                               hidT[s][:, 0], ALU.mult, ALU.subtract).then_inc(hid_ready, 1)

            def add_routed(c, r, slot, signal):
                for t in range(NT):
                    y = sum_rows(c)[:, t, :]
                    last = nc.vector.scalar_tensor_tensor(y, routed_row(slot, r, t), gate[:, r, bass.ds(c * NT + t, 1)], y,
                                                          ALU.mult, ALU.add)
                last.then_inc(signal, 1)

            def weigh(c, slot, m, n, half, done):
                dve.wait_ge(c_r_loaded[slot], K_TOP * NT * 16 * m)
                add_routed(c, 0, slot, half)
                dve.wait_ge(half, n)
                add_routed(c, 1, slot, done)

            def weigh_late(i, s, last=False):
                m = i - EARLY // 2 + 1
                dve.wait_ge(y_loaded[s], 16 * m)
                slot, nth = (2 + s, EARLY // 2 + 1) if last else (s, m)
                weigh(2 * i + s, slot, nth, 2 * i + s - EARLY + 1, half_weighed, weighed)

            def add_shared(c, first=False):
                if first:
                    dve.wait_ge(y_loaded[0], 16)
                else:
                    dve.wait_ge(weighed, c - EARLY + 1)
                for t in range(NT):
                    dve.wait_ge(down_ready, NT * c + t + 1)
                    y = sum_rows(c)[:, t, :]
                    nc.vector.scalar_tensor_tensor(y, DOWN[t][:], col(un_dn, SH_REST), y, ALU.mult, ALU.add).then_inc(shared_ready, 1)

            low_hid(EARLY, 0)
            low_condT(EARLY + 2, 0)
            low_hid(EARLY + 1, 1)
            add_shared(EARLY, first=True)
            dve.wait_ge(shared_ready, NT * EARLY + NT)
            weigh_late(EARLY // 2, 0)
            low_condT(EARLY + 3, 1)
            low_hid(EARLY + 2, 0)
            weigh_late(EARLY // 2, 1)
            with dve.Fori(EARLY // 2 + 1, A_HALF - 1) as i:
                for s in range(2):
                    c = 2 * i + s
                    add_shared(c - 1)
                    low_condT(c + 2, s)
                    dve.wait_ge(e_loaded[s], 16 * (i - EARLY // 2))
                    weigh(c - EARLY - 2, 2 + s, i - EARLY // 2, c - EARLY - 1, e_half_weighed, e_weighed)
                    low_hid(c + 1, 1 - s)
                    weigh_late(i, s)
            add_shared(NC - 3)
            low_hid(NC - 1, 1)
            weigh_late(A_HALF - 1, 0, last=True)
            add_shared(NC - 2)
            weigh_late(A_HALF - 1, 1, last=True)
            add_shared(NC - 1)

        @block.tensor
        def _(pe):
            mm = nc.tensor.matmul

            PASSES = ((0, 0), (0, 1), (1, 0))

            def cond_products(c, i, s, first=False, whole=False):
                if whole:
                    pe.wait_ge(act_loaded[s], 16 * (i + 1))
                else:
                    pe.wait_ge(x_split, c - 1)
                if not first:
                    pe.wait_ge(xam_ready, c)
                for k in range(HK):
                    for n, (ap, bp) in enumerate(PASSES[0:1] if whole else PASSES):
                        last = mm(XA[:, 0:CHUNK], at_in[:, k, :] if whole else at_[:, ap, k, :],
                                  act_in[s][:, k, :] if whole else xp[s][:, bp, k, :],
                                  start=(k == 0 and n == 0), stop=(k == HK - 1 and (whole or n == 2)))
                last.then_inc(xa_ready, 1)
                if first:
                    pe.wait_ge(w_cond, 3 * 16)
                for t in range(NT):
                    if not first:
                        pe.wait_ge(rows_ready, NT * c - NT + t + 1)
                    for k in range(HK):
                        for n, (ap, bp) in enumerate(PASSES[0:1] if whole else PASSES):
                            at = slice(t * P, (t + 1) * P)
                            last = mm(COND[t][:], act_in[s][:, k, at] if whole else xp[s][:, ap, k, at],
                                      w_in[:, k, :] if whole else wt[:, bp, k, :], start=(k == 0 and n == 0), stop=False)
                last.then_inc(act_used, 1)

            def adapter_products(c, s):
                pe.wait_ge(xam_ready, c + 1)
                for t in range(NT):
                    mm(COND[t][:], xam[s][:, t * P:(t + 1) * P], bmt, start=False, stop=True).then_inc(cond_ready, 1)

            def cond_transposes(c, s, first=False):
                for t in range(NT):
                    pe.wait_ge(rows_ready, NT * c + t + 1)
                    if not first:
                        pe.wait_ge(condT_ready, NT * c - NT + t + 1)
                    for k in range(HK):
                        last = nc.tensor.transpose(XPOSE[t][:, k * P:(k + 1) * P], rows[s][:, t, k * P:(k + 1) * P], ident[:])
                    last.then_inc(xpose_ready, 1)

            def router_products(c, s, first=False):
                pe.wait_ge(condT_ready, NT * c + NT)
                if not first:
                    pe.wait_ge(logit_copied, c)
                for t in range(NT):
                    for k in range(HK):
                        last = mm(LOGIT[:, t * E_RT:(t + 1) * E_RT], hid[s][:, k, t * P:(t + 1) * P], wr[:, k, :],
                                  start=(k == 0), stop=(k == HK - 1))
                last.then_inc(logit_ready, 1)

            def cond_step(c, i, s, first=False):
                cond_products(c, i, s, whole=first)
                cond_transposes(c - 1, 1 - s, first)
                adapter_products(c, s)
                router_products(c - 1, 1 - s, first)

            pe.wait_ge(w_adapters, 16)
            pe.wait_ge(consts, 2)
            cond_products(0, 0, 0, first=True, whole=True)
            adapter_products(0, 0)
            cond_step(1, 0, 1, first=True)
            pe.wait_ge(lin_split, 2)
            with pe.Fori(1, A_HALF) as i:
                cond_step(2 * i, i, 0)
                cond_step(2 * i + 1, i, 1)
            cond_transposes(NC - 1, 1)

            def prefix_products():
                pe.wait_ge(onehot_ready, 1)
                mm(PRE[:], lower[:], oh_sum[:].rearrange("p t e -> p (t e)"), start=True, stop=True)
                mm(TOT[:], ones[:], oh_sum[:].rearrange("p t e -> p (t e)"), start=True, stop=True).then_inc(prefix_ready, 1)

            def tile_expert_product():
                pe.wait_ge(tile_col_ready, 1)
                mm(TILE_E[0:1, 0:NJ_ALL + 2], tile_col[:], ident[:, 0:NJ_ALL + 2], start=True, stop=True).then_inc(tile_row_ready, 1)

            def inversion_products(g):
                pe.wait_ge(place_ready, g + 1)
                for n in range(GRP):
                    last = mm(INV[:, 0:NJ_ALL], in_part[g % 2][:, n, :], in_val[g % 2][:, n, :],
                              start=(g == 0 and n == 0), stop=(g == NG - 1 and n == GRP - 1))
                last.then_inc(place_used, 1)

            def shared_up(i, s, first=False, blocks=range(EM)):
                c = 2 * i + s
                pe.wait_ge(actT_ready, c + 1)
                for em in blocks:
                    e, m = em // DM, em % DM
                    if not (first and em < 2):
                        pe.wait_ge(gelu_ready, EM * c + em - 1)
                    for k in range(HK):
                        for n, (wp, xp) in enumerate(PASSES):
                            w0 = (UP_HI, UP_LO)[wp] + k * D + m * P
                            last = mm(UP[em % 2][:, 0:CHUNK], shw[:, e, w0:w0 + P], actT[s][:, xp, k, :],
                                      start=(k == 0 and n == 0), stop=(k == HK - 1 and n == 2))
                    last.then_inc(up_ready, 1)

            def shared_down(i, s, first=False):
                c = 2 * i + s
                pe.wait_ge(hid_ready, c + 1)
                for t in range(NT):
                    if not first:
                        pe.wait_ge(shared_ready, NT * c - NT + t + 1)
                    for em in range(EM):
                        for n, (xp, wp) in enumerate(PASSES):
                            w0 = (DN_HI, DN_LO)[wp] + em % DM * H
                            last = mm(DOWN[t][:], hidT[s][:, xp, em, t * P:(t + 1) * P], shw[:, em // DM, w0:w0 + H],
                                      start=(em == 0 and n == 0), stop=(em == EM - 1 and n == 2))
                    last.then_inc(down_ready, 1)

            pe.wait_ge(w_split, 2)
            pe.wait_ge(rows_ready, TT)
            shared_up(0, 0, first=True)
            router_products(NC - 1, 1)
            shared_up(0, 1)
            prefix_products()
            shared_down(0, 0, first=True)
            shared_up(1, 0)
            tile_expert_product()
            shared_down(0, 1)
            shared_up(1, 1)
            inversion_products(0)
            shared_down(1, 0)
            inversion_products(1)
            inversion_products(2)
            shared_up(2, 0)
            inversion_products(3)
            inversion_products(4)
            shared_down(1, 1)
            inversion_products(5)
            inversion_products(6)
            shared_up(2, 1, blocks=range(2))
            inversion_products(7)
            shared_up(2, 1, blocks=range(2, EM))
            shared_down(2, 0)

            def r_transpose_x(j, i, s, first=False):
                pe.wait_ge(xg_loaded[s], 16 * (i + 1))
                if not first:
                    pe.wait_ge(xgT_ready, j - 1)
                for k in range(HK):
                    last = nc.tensor.transpose(R_XT[s][:, k * P:(k + 1) * P], xg[s][:, k * P:(k + 1) * P], ident[:])
                last.then_inc(xgT_psum, 1)

            def r_experts(i):
                return nc.values_load_multi_w_load_instructions(
                    tile_e[0:1, bass.ds(i, 1), 0:3].rearrange("p a m -> p (a m)"), engines=(mybir.EngineType.PE,), min_val=0, max_val=E_RT - 1,
                    skip_runtime_bounds_check_because="a count of experts, cut off at the last one by the vector engine")[1]

            def r_up(j, s, e, first=False):
                pe.wait_ge(xgT_ready, j + 1)
                if not first:
                    pe.wait_ge(r_gelu_ready, j - 1)
                for k in range(HK):
                    for n, (xp, wp) in enumerate(PASSES):
                        w0 = (UP_HI, UP_LO)[wp] + k * D
                        last = mm(R_UP[s][:, 0:D], xgT[s][:, xp, k, :], rtw[:, bass.ds(e, 1), w0:w0 + D].rearrange("p a d -> p (a d)"),
                                  start=(k == 0 and n == 0), stop=(k == HK - 1 and n == 2))
                last.then_inc(r_up_ready, 1)

            def r_transpose_mid(j, s, first=False):
                pe.wait_ge(r_gelu_ready, j + 1)
                if not first:
                    pe.wait_ge(midT_ready, j - 1)
                for m in range(DM):
                    last = nc.tensor.transpose(R_MT[s][:, m * P:(m + 1) * P], mid[s][:, m * P:(m + 1) * P], ident[:])
                last.then_inc(midT_psum, 1)

            def r_down(j, s, e, first=False):
                pe.wait_ge(midT_ready, j + 1)
                if not first:
                    pe.wait_ge(rrow_ready, j - 1)
                for m in range(DM):
                    for n, (xp, wp) in enumerate(PASSES):
                        w0 = (DN_HI, DN_LO)[wp] + m * H
                        last = mm(R_DN[s][:], midT[s][:, xp, m, :], rtw[:, bass.ds(e, 1), w0:w0 + H].rearrange("p a h -> p (a h)"),
                                  start=(m == 0 and n == 0), stop=(m == DM - 1 and n == 2))
                last.then_inc(r_dn_ready, 1)

            pe.wait_ge(w_split, SPLITS)
            pe.wait_ge(sorted_ready, 1)
            pe.wait_ge(gelu_ready, EM * EARLY)
            def r_pair(i, first=False, more=True):
                e = r_experts(i)
                for s in range(2):
                    j = 2 * i + s
                    r_transpose_mid(j, s, first and i == 0)
                    r_up(j + 1, 1 - s, e[s + 1], first and i == 0 and s == 0)
                    if more:
                        r_transpose_x(j + 3, i + 1 + s, 1 - s)
                    if first and i == 0 and s == 0:
                        pe.wait_ge(shared_ready, NT * EARLY)
                    r_down(j, s, e[s], first and i == 0)

            for s in range(2):
                r_transpose_x(s, 0, s, first=True)
            shared_down(2, 1)
            r_up(0, 0, r_experts(0)[0], first=True)
            r_transpose_x(2, 1, 0)
            for i in range(2):
                r_pair(i, first=True)
            with pe.Fori(2, NJ_2 - 1) as i:
                r_pair(i)
            r_pair(NJ_2 - 1, more=False)
            e = r_experts(NJ_2)
            r_transpose_mid(NJ - 1, 0)
            shared_up(EARLY // 2, 0, blocks=range(1))
            r_down(NJ - 1, 0, e[0])
            shared_up(EARLY // 2, 0, blocks=range(1, EM))
            pe.wait_ge(rrow_ready, NJ)
            with pe.Fori(EARLY // 2, A_HALF - 1) as i:
                shared_up(i, 1)
                shared_down(i, 0)
                shared_up(i + 1, 0)
                shared_down(i, 1)
            shared_up(A_HALF - 1, 1)
            shared_down(A_HALF - 1, 0)
            shared_down(A_HALF - 1, 1)


def kernel(x, itok_B_0_6, L0_cond_W, L0_cond_A, L0_cond_Bm, L0_cond_scalings, L0_ffn_Wsh_up, L0_ffn_Wsh_down,
           L0_ffn_Wrt_up, L0_ffn_Wrt_down, L0_ffn_W_router):
    import numpy as np
    import concourse.bacc as bacc
    from concourse.bass_utils import run_bass_kernel_spmd

    def blocks(w, e, k, n):
        return np.ascontiguousarray(np.asarray(w).reshape(e, k, P, n).transpose(2, 0, 1, 3))

    x = np.asarray(x)
    a = np.asarray(L0_cond_A).reshape(AR, H)
    arrays = {
        "xT": np.ascontiguousarray(x.reshape(NC, CHUNK, HK, P).transpose(0, 3, 2, 1)).reshape(NC, P, HK * CHUNK),
        "x_rows": np.ascontiguousarray(x.reshape(TOK, H)),
        "idx": np.asarray(itok_B_0_6),
        "WT": blocks(np.asarray(L0_cond_W).T, 1, HK, H)[:, 0],
        "AT": blocks(a.T, 1, HK, AR)[:, 0],
        "BmT": np.ascontiguousarray(np.asarray(L0_cond_Bm).transpose(0, 2, 1)).reshape(AR, H),
        "scal": np.repeat(np.asarray(L0_cond_scalings), RANK).reshape(AR, 1),
        "sh_up": blocks(L0_ffn_Wsh_up, E_SH, HK, D).reshape(P, E_SH * WU),
        "sh_dn": blocks(L0_ffn_Wsh_down, E_SH, DM, H).reshape(P, E_SH * WD),
        "rt_w": np.concatenate([blocks(L0_ffn_Wrt_up, E_RT, HK, D).reshape(P, E_RT, WU),
                                blocks(L0_ffn_Wrt_down, E_RT, DM, H).reshape(P, E_RT, WD)], axis=2),
        "w_r": blocks(L0_ffn_W_router, 1, HK, E_RT)[:, 0],
    }
    arrays = {name: np.ascontiguousarray(v) for name, v in arrays.items()}
    nc = bacc.Bacc("TRN2", target_bir_lowering=False, num_devices=1)
    args = [nc.dram_tensor(name, v.shape, mybir.dt.from_np(v.dtype), kind="ExternalInput").ap()
            for name, v in arrays.items()]
    out = nc.dram_tensor("out", [TOK, H], F32, kind="ExternalOutput").ap()
    adaln_moe_kernel(nc, *args, out)
    r = run_bass_kernel_spmd(nc, [arrays], core_ids=[0])
    return r.results[0]["out"].reshape(B, S, H)
```
